# Optimizing a Trainium2 kernel written in Bass

```python
import numpy as np
import jax
import jax.numpy as jnp

def _softmax(x, axis=-1):
    return jax.nn.softmax(x, axis=axis)

def _gelu(x):
    return jax.nn.gelu(x, approximate=True)

def _silu(x):
    return jax.nn.silu(x)

def _sigmoid(x):
    return jax.nn.sigmoid(x)

def _layernorm(x, axis=-1, eps=1e-05):
    m = jnp.mean(x, axis=axis, keepdims=True)
    v = jnp.var(x, axis=axis, keepdims=True)
    return (x - m) / jnp.sqrt(v + eps)

def _scatter_add(tgt, idx, src, axis=0):
    return tgt.at[idx].add(src)

def _segment_sum(src, seg, n):
    return jax.ops.segment_sum(src, seg, n)
kernel_name = 'mk_seq_preln_d1_jaxref_r8_16ceb5'

def setup_inputs(seed: int=0):
    np.random.seed(seed)
    _w = jnp.asarray

    def _L0_attn_setup():
        import jax, jax.numpy as jnp
        import numpy as np
        CHUNK = 64
        LR = 0.001

        def _fast_weight(xc, a0, a1, a2):
            h = jax.nn.silu(jnp.einsum('bch,hf->bcf', xc, a0)) * jnp.einsum('bch,hf->bcf', xc, a2)
            return jnp.einsum('bcf,fh->bch', h, a1)

        def _reference_tuple_inner(x, w0, w1, w2):
            B, S, H = x.shape
            nC = S // CHUNK
            xc = x.reshape(B, nC, CHUNK, H).transpose(1, 0, 2, 3)

            def step(carry, x_chunk):
                a0, a1, a2, acc_loss = carry
                out = _fast_weight(x_chunk, a0, a1, a2)
                chunk_loss = jnp.mean((out - x_chunk) ** 2)
                decay = 1.0 - LR * chunk_loss
                return ((a0 * decay, a1 * decay, a2 * decay, acc_loss + chunk_loss), out)
            init = (w0, w1, w2, jnp.float32(0.0))
            (_, _, _, total_loss), outs = jax.lax.scan(step, init, xc)
            output = outs.transpose(1, 0, 2, 3).reshape(B, S, H)
            return (output, total_loss / nC)
        key = jax.random.key(seed)
        k1, k2, k3, k4 = jax.random.split(key, 4)
        B, S, H, F = (4, 512, 128, 512)
        x = jax.random.normal(k1, (B, S, H), dtype=jnp.float32)
        w0 = jax.random.normal(k2, (H, F), dtype=jnp.float32) * 0.02
        w1 = jax.random.normal(k3, (F, H), dtype=jnp.float32) * 0.02
        w2 = jax.random.normal(k4, (H, F), dtype=jnp.float32) * 0.02
        return {'x': x, 'w0': w0, 'w1': w1, 'w2': w2}
    _L0_attn_in = _L0_attn_setup()

    def _L0_ffn_setup():
        import math
        import jax, jax.numpy as jnp
        import numpy as np
        E = 8
        K = 2
        CF = 1.25
        D = 128
        F = 256
        B, S = (4, 256)
        key = jax.random.key(seed)
        ks = jax.random.split(key, 8)
        sd = 1.0 / math.sqrt(D)
        sf = 1.0 / math.sqrt(F)
        return {'x': jax.random.normal(ks[0], (B, S, D), jnp.float32), 'router_w': jax.random.normal(ks[1], (D, E), jnp.float32) * sd, 'router_b': jnp.zeros((E,), jnp.float32), 'w1': jax.random.normal(ks[2], (E, D, F), jnp.float32) * sd, 'b1': jax.random.normal(ks[3], (E, F), jnp.float32) * 0.01, 'w2': jax.random.normal(ks[4], (E, F, D), jnp.float32) * sf, 'b2': jax.random.normal(ks[5], (E, D), jnp.float32) * 0.01}
    _L0_ffn_in = _L0_ffn_setup()
    _d = {'L0_attn_x': _L0_attn_in['x'], 'L0_attn_w0': _L0_attn_in['w0'], 'L0_attn_w1': _L0_attn_in['w1'], 'L0_attn_w2': _L0_attn_in['w2'], 'L0_ffn_router_w': _L0_ffn_in['router_w'], 'L0_ffn_router_b': _L0_ffn_in['router_b'], 'L0_ffn_w1': _L0_ffn_in['w1'], 'L0_ffn_b1': _L0_ffn_in['b1'], 'L0_ffn_w2': _L0_ffn_in['w2'], 'L0_ffn_b2': _L0_ffn_in['b2']}
    _x0 = _d['L0_attn_x']
    _d['L0_attn_x'] = jax.random.normal(jax.random.fold_in(jax.random.key(seed), 1), (4, 512, 128), dtype=_x0.dtype)
    del _x0
    return _d

def reference(L0_attn_x, L0_attn_w0, L0_attn_w1, L0_attn_w2, L0_ffn_router_w, L0_ffn_router_b, L0_ffn_w1, L0_ffn_b1, L0_ffn_w2, L0_ffn_b2):

    def _L0_attn_ref(x, w0, w1, w2):
        import jax, jax.numpy as jnp
        import numpy as np
        CHUNK = 64
        LR = 0.001

        def _fast_weight(xc, a0, a1, a2):
            h = jax.nn.silu(jnp.einsum('bch,hf->bcf', xc, a0)) * jnp.einsum('bch,hf->bcf', xc, a2)
            return jnp.einsum('bcf,fh->bch', h, a1)

        def _reference_tuple_inner(x, w0, w1, w2):
            B, S, H = x.shape
            nC = S // CHUNK
            xc = x.reshape(B, nC, CHUNK, H).transpose(1, 0, 2, 3)

            def step(carry, x_chunk):
                a0, a1, a2, acc_loss = carry
                out = _fast_weight(x_chunk, a0, a1, a2)
                chunk_loss = jnp.mean((out - x_chunk) ** 2)
                decay = 1.0 - LR * chunk_loss
                return ((a0 * decay, a1 * decay, a2 * decay, acc_loss + chunk_loss), out)
            init = (w0, w1, w2, jnp.float32(0.0))
            (_, _, _, total_loss), outs = jax.lax.scan(step, init, xc)
            output = outs.transpose(1, 0, 2, 3).reshape(B, S, H)
            return (output, total_loss / nC)
        return _reference_tuple_inner(x, w0, w1, w2)[0]

    def _L0_ffn_ref(x, router_w, router_b, w1, b1, w2, b2):
        import math
        import jax, jax.numpy as jnp
        import numpy as np
        E = 8
        K = 2
        CF = 1.25
        D = 128
        F = 256
        B, S = (4, 256)
        b, s, d = x.shape
        xf = x.reshape(-1, d)
        T = b * s
        A = T * K
        cap = max(1, int(math.ceil(CF * A / E)))
        logits = xf @ router_w + router_b
        probs = jax.nn.softmax(logits, axis=-1)
        topk_p, topk_i = jax.lax.top_k(probs, K)
        topk_p = topk_p / jnp.clip(topk_p.sum(-1, keepdims=True), 1e-09)
        a_tok = jnp.repeat(jnp.arange(T), K)
        a_exp = topk_i.reshape(-1)
        a_w = topk_p.reshape(-1)
        order = jnp.argsort(a_exp)
        se, st, sw = (a_exp[order], a_tok[order], a_w[order])
        counts = jnp.bincount(se, length=E)
        starts = jnp.cumsum(counts) - counts
        rank = jnp.arange(A) - starts[se]
        keep = rank < cap
        slot = jnp.where(keep, se * cap + rank, E * cap)
        buf = jnp.zeros((E * cap + 1, d), x.dtype).at[slot].set(xf[st])
        buf = buf[:-1].reshape(E, cap, d)
        h = jax.nn.gelu(jnp.einsum('ecd,edf->ecf', buf, w1) + b1[:, None, :], approximate=False)
        eo = jnp.einsum('ecf,efd->ecd', h, w2) + b2[:, None, :]
        eo_flat = jnp.concatenate([eo.reshape(E * cap, d), jnp.zeros((1, d), x.dtype)], axis=0)
        w = jnp.where(keep, sw, 0.0)[:, None]
        out = jnp.zeros_like(xf).at[st].add(eo_flat[slot] * w)
        return out.reshape(b, s, d)
    x = L0_attn_x
    x = x + _L0_attn_ref(_layernorm(x, axis=-1), L0_attn_w0, L0_attn_w1, L0_attn_w2)
    x = x + _L0_ffn_ref(_layernorm(x, axis=-1), L0_ffn_router_w, L0_ffn_router_b, L0_ffn_w1, L0_ffn_b1, L0_ffn_w2, L0_ffn_b2)
    return x

_drawn_inputs = setup_inputs


def setup_inputs(seed=0):
    import zlib

    import numpy as np

    out = dict(_drawn_inputs(seed))
    spreads = {'L0_ffn_router_b': (0.0, 0.1)}
    factors = {'L0_ffn_b1': 8.0, 'L0_ffn_b2': 8.0}
    for name, (base, spread) in spreads.items():
        noise = np.random.default_rng([zlib.crc32(name.encode()), seed]).standard_normal(out[name].shape)
        drawn = base * np.exp(spread * noise) if base else spread * noise
        out[name] = jnp.asarray(drawn.astype(out[name].dtype))
    for name, factor in factors.items():
        out[name] = (out[name] * factor).astype(out[name].dtype)
    return out
```

```python
from contextlib import ExitStack

import concourse.bass as bass
from concourse import mybir

ALU = mybir.AluOpType
ACT = mybir.ActivationFunctionType
AX = mybir.AxisListType
F32 = mybir.dt.float32
BF16 = mybir.dt.bfloat16
I32 = mybir.dt.int32
U32 = mybir.dt.uint32

P = 128
CHUNK = 64
LR = 0.001
EPS = 1e-5
TOP = 2
ROW = P + 4
DEST, GATE = P, P + 1
NOWHERE = 1.0e6


def block_kernel(nc, x, w0, w1, w2, router_w, router_b, we1, be1, we2, be2, out):
    B, S, D = x.shape
    F = w0.shape[1]
    E = router_w.shape[1]
    EF = we1.shape[2]
    NC = S // CHUNK
    NM = B * CHUNK // P
    CT = NM * P
    NF = F // P
    NEF = EF // P
    T = B * S
    CAP = -(-5 * T * TOP // (4 * E))
    NJ = CAP // P
    assert D == P and NM == 2 and CAP % P == 0 and NC % 2 == 0 and E == 8
    SOON = 3 * NM
    HALVES = ((0, 3 * P), (3 * P, CAP))
    DOWN = ((0, 3), (3, NJ))
    PIECES = [(m, lo, lo + NC // 2) for m in range(NM) for lo in (0, NC // 2)]

    slots = nc.dram_tensor("slots", [E * CAP, ROW], F32).ap()
    rows_kept = nc.dram_tensor("rows_kept", [NC, P, NM * TOP * ROW], F32).ap()
    chosen = nc.dram_tensor("chosen", [T * TOP, P], F32).ap()

    with ExitStack() as ctx:
        def sb(name, shape, dt=F32):
            return ctx.enter_context(nc.sbuf_tensor(name, shape, dt))

        def ps(name, shape):
            return ctx.enter_context(nc.psum_tensor(name, shape, F32))

        def sem(name):
            return ctx.enter_context(nc.semaphore(name))

        ident = sb("ident", [P, P])
        earlier = sb("earlier", [P, P], BF16)
        same_or_earlier_row = sb("same_or_earlier_row", [P, P], BF16)
        earlier_row = sb("earlier_row", [P, P], BF16)
        ones = sb("ones", [P, P], BF16)
        ones_row = sb("ones_row", [1, P])
        loss_w = sb("loss_w", [P, P])
        expert_id = sb("expert_id", [P, NM * TOP, E])
        expert_base = sb("expert_base", [P, NM, E])
        nowhere = sb("nowhere", [P, NC * NM, E])
        dest_id = sb("dest_id", [P, NC, NM, TOP])
        minus_half = sb("minus_half", [P, NC * NM])
        blank = sb("blank", [P, NJ, ROW])
        ints = sb("ints", [P, NC * NM * TOP], I32)
        w0_sb = sb("w0_sb", [P, F])
        w2_sb = sb("w2_sb", [P, F])
        w1_sb = sb("w1_sb", [P, NF, P])
        rw_sb = sb("rw_sb", [P, E])
        rb_sb = sb("rb_sb", [1, E])
        x_all = sb("x_all", [P, NC, NM, P])
        xn_all = sb("xn_all", [P, NC, NM, P])
        xnT_all = sb("xnT_all", [P, NC, CT])
        x1_all = sb("x1_all", [P, NC, NM, P])
        stats1 = sb("stats1", [P, NC * NM, 6])
        mv1 = sb("mv1", [P, NC * NM, 2])
        var1 = sb("var1", [P, NC * NM])
        rstd1 = sb("rstd1", [P, NC * NM])
        shift1 = sb("shift1", [P, NC * NM])
        gated = sb("gated", [P, NF, CT])
        prod = sb("prod", [P, NF, CT])
        s_cur = sb("s_cur", [P, 2])
        s_sq = sb("s_sq", [P, 2])
        diff = sb("diff", [P, NM, P])
        junk = sb("junk", [P, NM, P])
        sq_sum = sb("sq_sum", [P, 1])
        stats2 = sb("stats2", [P, NM, 6])
        mv2 = sb("mv2", [P, NM, 2])
        var2 = sb("var2", [P, NM])
        rstd2 = sb("rstd2", [P, NM])
        shift2 = sb("shift2", [P, NM])
        minus_mean2 = sb("minus_mean2", [P, NM])
        rows = sb("rows", [P, 2, NM, TOP, ROW])
        zT = sb("zT", [P, CT])
        best = sb("best", [P, NM, 8])
        best_id = sb("best_id", [P, NM, 8], U32)
        gap = sb("gap", [P, NM])
        half_tanh = sb("half_tanh", [P, NM])
        pick_all = sb("pick_all", [P, NC, NM, TOP, E])
        mask_all = sb("mask_all", [P, NC, NM, E], BF16)
        before_all = sb("before_all", [P, NC + 1, NM, E], BF16)
        after_all = sb("after_all", [P, NC, NM, E], BF16)
        over = sb("over", [P, NM, E])
        based = sb("based", [P, NM, E])
        slot_of = sb("slot_of", [P, NM, E])
        slot_pick = sb("slot_pick", [P, NM, TOP, E])
        slot_f = sb("slot_f", [P, NM * TOP])
        slot_i = sb("slot_i", [P, 2, NM * TOP], I32)
        most = sb("most", [P, 1])
        overflow = sb("overflow", [P, 1], I32)
        over_l = sb("over_l", [P, NC * NM, E])
        based_l = sb("based_l", [P, NC * NM, E])
        pick_l = sb("pick_l", [P, NC * NM, TOP, E])
        slot_fl = sb("slot_fl", [P, NC * NM * TOP])
        slot_il = sb("slot_il", [P, NC, NM * TOP], I32)
        again_i = sb("again_i", [P, NM * TOP], I32)
        again_rows = sb("again_rows", [P, NM, TOP, ROW])
        b1_rows = sb("b1_rows", [E * NEF, P])
        b1T = sb("b1T", [P, E * NEF])
        b2_sb = sb("b2_sb", [P, E, P])
        we1_sb = sb("we1_sb", [P, 2, EF])
        we2_sb = sb("we2_sb", [P, 2, NEF, P])
        xs = sb("xs", [P, 2, NJ, ROW])
        xsT = sb("xsT", [P, CAP])
        hidden = sb("hidden", [P, NEF, CAP])
        dst = sb("dst", [P, 2, NJ], I32)
        wgt = sb("wgt", [P, 2, NJ])
        biased = sb("biased", [P, NJ, P])
        result = sb("result", [P, 2, NJ, P])
        picked = sb("picked", [P, NM, NC, TOP * P])
        summed = sb("summed", [P, NM, NC, P])
        final = sb("final", [P, NM, NC, P])

        gu = ps("gu", [P, 2, NF, CT])
        turned = ps("turned", [P, 2, 512])
        outp = ps("outp", [P, 2, 512])
        zT_ps = turned[:, 0, 0:CT]
        loss_ps = turned[:, 1, 0:1]
        b1T_ps = turned[:, 0, 0:E * NEF]
        count_ps = turned[:, 1, 0:E]
        out_ps = outp[:, 0, 0:NM * P].rearrange("p (m d) -> p m d", d=P)
        logits_ps = outp[:, 1, 0:NM * E].rearrange("p (m e) -> p m e", e=E)
        pos_ps = outp[:, 1, 32:32 + NM * E].rearrange("p (m e) -> p m e", e=E)
        rank_ps = outp[:, 0, 0:NC * NM * E].rearrange("p (c m e) -> p c m e", m=NM, e=E)
        hid_ps = gu[:, :, :, :].rearrange("p a f t -> p (a f t)").rearrange("p (b n) -> p b n", n=512)
        xsT_ps = turned[:, :, :].rearrange("p a n -> p (a n)")[:, 0:CAP]
        eo_ps = outp[:, :, :].rearrange("p a (j d) -> p a j d", d=P)

        x_first, x_rest, w_up, w_down, w_route, b_exp = (sem(n) for n in (
            "x_first", "x_rest", "w_up", "w_down", "w_route", "b_exp"))
        blank_made, slots_blank = sem("blank_made"), sem("slots_blank")
        const_step, const_ready = sem("const_step"), sem("const_ready")
        ln1_step, mv1_ready, rstd1_step = sem("ln1_step"), sem("mv1_ready"), sem("rstd1_step")
        rstd1_ready, xn_first, xn_rest = sem("rstd1_ready"), sem("xn_first"), sem("xn_rest")
        shift1_ready, xn_soon = sem("shift1_ready"), sem("xn_soon")
        xT_in_psum, xT_ready = sem("xT_in_psum"), sem("xT_ready")
        b1_in_psum, b1_ready = sem("b1_in_psum"), sem("b1_ready")
        g_ready, u_ready, gated_ready, prod_ready = sem("g_ready"), sem("u_ready"), sem("gated_ready"), sem("prod_ready")
        out_ready, diff_ready, x1_ready = sem("out_ready"), sem("diff_ready"), sem("x1_ready")
        sq_ready, loss_ready, s_ready, s_sq_ready = sem("sq_ready"), sem("loss_ready"), sem("s_ready"), sem("s_sq_ready")
        stats2_done, mv2_ready, rstd2_step, rstd2_ready = (sem(n) for n in (
            "stats2_done", "mv2_ready", "rstd2_step", "rstd2_ready"))
        shift2_ready, z_ready, rows_ready, zT_in_psum, zT_ready, logits_in_psum = (sem(n) for n in (
            "shift2_ready", "z_ready", "rows_ready", "zT_in_psum", "zT_ready", "logits_in_psum"))
        best_ready, best_id_ready, gap_ready, tanh_ready, pick_ready, mask_ready = (sem(n) for n in (
            "best_ready", "best_id_ready", "gap_ready", "tanh_ready", "pick_ready", "mask_ready"))
        pos_ready, slot_step, slot_picked, slot_ready, before_ready, meta_ready = (sem(n) for n in (
            "pos_ready", "slot_step", "slot_picked", "slot_ready", "before_ready", "meta_ready"))
        rows_stored = [sem(f"rows_stored{q}") for q in range(2)]
        rows_sent = [sem(f"rows_sent{q}") for q in range(2)]
        count_ready, most_ready, overflow_ready = sem("count_ready"), sem("most_ready"), sem("overflow_ready")
        after_step, after_ready, rank_ready = sem("after_step"), sem("after_ready"), sem("rank_ready")
        late_step, late_slots = sem("late_step"), sem("late_slots")
        cleared, again_loaded, again_copied, again_sent = (sem(n) for n in (
            "cleared", "again_loaded", "again_copied", "again_sent"))
        dispatched = sem("dispatched")
        settled = {k: sem(f"settled_{k}") for k in ("pool", "act", "dve")}
        xs_loaded = [sem(f"xs_loaded{q}") for q in range(2)]
        we_loaded = [sem(f"we_loaded{q}") for q in range(2)]
        xs_read, xsT_in_psum, xsT_ready = sem("xs_read"), sem("xsT_in_psum"), sem("xsT_ready")
        hid_in_psum, hid_ready, eo_in_psum = sem("hid_in_psum"), sem("hid_ready"), sem("eo_in_psum")
        biased_ready, result_ready = sem("biased_ready"), sem("result_ready")
        result_sent = [sem(f"result_sent{q}") for q in range(2)]
        picked_loaded = [sem(f"picked_loaded{m}") for m in range(len(PIECES))]
        summed_ready, final_ready, out_stored = sem("summed_ready"), sem("final_ready"), sem("out_stored")

        def one(ap, i):
            v = ap[:, bass.ds(i, 1)]
            names = "abcd"[:len(v.shape) - 2]
            if not names:
                return v
            return v.rearrange(f"p o {' '.join(names)} -> p (o {names[0]}) {' '.join(names[1:])}")

        def by_expert(step):
            def run(eng, n):
                step(0, 0, 0)
                step(1, 1, 0)
                with eng.Fori(0, n // 2 - 1) as i:
                    step(2 * i + 2, 0, i + 1)
                    step(2 * i + 3, 1, i + 1)
            return run

        def by_expert_ahead(step):
            def run(eng, n):
                step(0, 0, 0)
                step(1, 1, 0)
                with eng.Fori(0, n // 2 - 2) as i:
                    step(2 * i + 2, 0, i + 1)
                    step(2 * i + 3, 1, i + 1)
                step(n - 2, 0, n // 2 - 1)
                step(n - 1, 1, n // 2 - 1)
            return run

        def first(c):
            return isinstance(c, int) and c == 0

        def second(c):
            return isinstance(c, int) and c == 1

        def pairs_before(c):
            return not (first(c) or second(c))

        def settle(eng, who):
            eng.sem_inc(settled[who], 1)

        block = ctx.enter_context(nc.Block())

        @block.sync
        def _(sp):
            def token_rows(t, b):
                return t[b].rearrange("(c s) d -> s c d", s=CHUNK)

            for h in range(2):
                part = slice(h * CHUNK, (h + 1) * CHUNK)
                sp.dma_start(x_all[part, 0, :, :],
                             x[h::2, 0:CHUNK, :].rearrange("m s d -> s m d")).then_inc(x_first, 16)
            sp.dma_start(w0_sb[:, :], w0).then_inc(w_up, 16)
            sp.dma_start(w2_sb[:, :], w2).then_inc(w_up, 16)
            for b in range(B):
                part = slice((b % 2) * CHUNK, (b % 2 + 1) * CHUNK)
                sp.dma_start(x_all[part, 1:NC, b // 2, :], token_rows(x, b)[:, 1:NC, :]).then_inc(x_rest, 16)
            sp.dma_start(w1_sb[:, :, :], w1.rearrange("(f p) d -> p f d", p=P)).then_inc(w_down, 16)
            sp.dma_start(rw_sb[:, :], router_w).then_inc(w_route, 16)
            sp.dma_start(rb_sb[:, :], router_b.rearrange("(o e) -> o e", o=1)).then_inc(w_route, 16)
            sp.dma_start(b1_rows[:, :], be1.rearrange("e (f p) -> (e f) p", p=P)).then_inc(b_exp, 16)
            sp.wait_ge(blank_made, 2)
            sp.dma_start(slots.rearrange("(e p j) r -> p e (j r)", p=P, j=NJ),
                         blank[:, :, :].rearrange("p (o j) r -> p o (j r)", o=1).to_broadcast([P, E, NJ * ROW]))\
                .then_inc(slots_blank, 16)
            sp.dma_start(b2_sb[:, :, :].rearrange("p e d -> p (e d)"),
                         be2.rearrange("(o e) d -> o (e d)", o=1).to_broadcast([P, E * D])).then_inc(b_exp, 16)

            def load_expert(e, q):
                sp.dma_start(we1_sb[:, q], we1[bass.ds(e, 1)].rearrange("o d f -> (o d) f")).then_inc(we_loaded[q], 16)
                sp.dma_start(we2_sb[:, q], we2[bass.ds(e, 1)].rearrange("o (f p) d -> p (o f) d", p=P))\
                    .then_inc(we_loaded[q], 16)

            load_expert(0, 0)
            load_expert(1, 1)

            def keep_rows(c, q, pairs):
                sp.wait_ge(rows_ready, 2 * c + 2)
                sp.wait_ge(meta_ready, 2 * c + 2)
                sp.dma_start(rows_kept[bass.ds(c, 1)].rearrange("o p n -> (o p) n"),
                             rows[:, q].rearrange("p m k r -> p (m k r)")).then_inc(rows_stored[q], 16)

            for c in range(NC):
                keep_rows(c, c % 2, c // 2)

            sp.wait_ge(dispatched, 1)

            def load_slots(e, q, pairs):
                if not isinstance(e, int):
                    sp.wait_ge(xsT_in_psum, e - 1)
                    sp.wait_ge(xs_read, 2 * e - 2)
                sp.dma_start(xs[:, q], slots[bass.ds(e * CAP, CAP), :].rearrange("(p j) r -> p j r", j=NJ))\
                    .then_inc(xs_loaded[q], 16)
                if not isinstance(e, int):
                    sp.wait_ge(eo_in_psum, 2 * e - 2)
                    load_expert(e, q)

            by_expert(load_slots)(sp, E)

            for q in range(2):
                sp.wait_ge(result_sent[q], 16 * NJ * (E // 2))
            by_token = chosen.rearrange("(b c s k) d -> b s c (k d)", b=B, c=NC, k=TOP)
            for n, (m, lo, hi) in enumerate(PIECES):
                for h in range(2):
                    sp.dma_start(picked[h * CHUNK:(h + 1) * CHUNK, m, lo:hi, :], by_token[2 * m + h][:, lo:hi, :])\
                        .then_inc(picked_loaded[n], 16)
            for n, (m, lo, hi) in enumerate(PIECES):
                sp.wait_ge(final_ready, n + 1)
                for h in range(2):
                    sp.dma_start(token_rows(out, 2 * m + h)[:, lo:hi, :],
                                 final[h * CHUNK:(h + 1) * CHUNK, m, lo:hi, :]).then_inc(out_stored, 16)
            sp.wait_ge(out_stored, 32 * len(PIECES))

        @block.gpsimd
        def _(pool):
            pool.memset(blank[:, :, :], 0.0).then_inc(blank_made, 1)
            pool.wait_ge(blank_made, 1)
            pool.memset(blank[:, :, DEST:DEST + 1], NOWHERE).then_inc(blank_made, 1)
            pool.memset(minus_half[:, :], -0.5)
            pool.memset(ident[:, :], 0.0).then_inc(const_step, 1)
            pool.memset(earlier[:, :], 1.0).then_inc(const_step, 1)
            pool.wait_ge(const_step, 2)
            pool.affine_select(out=ident[:, :], in_=ident[:, :], compare_op=ALU.not_equal, fill=1.0,
                               base=0, pattern=[[-1, P]], channel_multiplier=1)
            pool.affine_select(out=earlier[:, :], in_=earlier[:, :], compare_op=ALU.is_ge, fill=0.0,
                               base=-1, pattern=[[1, P]], channel_multiplier=-1).then_inc(const_ready, 1)

            def rstd_of(lo, hi, n):
                pool.wait_ge(mv1_ready, hi)
                pool.tensor_scalar(var1[:, lo:hi], mv1[:, lo:hi, 1], EPS, None, ALU.add).then_inc(rstd1_step, 1)
                pool.wait_ge(rstd1_step, n)
                pool.tensor_tensor(rstd1[:, lo:hi], var1[:, lo:hi], minus_half[:, lo:hi], ALU.pow)\
                    .then_inc(rstd1_ready, 1)

            rstd_of(0, NM, 1)
            pool.memset(loss_w[:, :], -LR / (CT * D))
            pool.memset(ones[:, :], 1.0)
            pool.memset(ones_row[:, :], 1.0)
            pool.memset(before_all[:, 0], 0.0)
            pool.memset(nowhere[:, :, :], NOWHERE)
            pool.memset(rows[:, :, :, :, P:ROW], 0.0).then_inc(const_ready, 1)
            rstd_of(NM, SOON, 2)
            rstd_of(SOON, NC * NM, 3)
            steps = [2]

            def stepped(ins):
                steps[0] += 1
                ins.then_inc(const_step, 1)
                pool.wait_ge(const_step, steps[0])

            stepped(pool.memset(same_or_earlier_row[:, :], 1.0))
            stepped(pool.memset(earlier_row[:, :], 0.0))
            stepped(pool.memset(same_or_earlier_row[CHUNK:P, 0:CHUNK], 0.0))
            stepped(pool.memset(earlier_row[0:CHUNK, CHUNK:P], 1.0))
            stepped(pool.iota(ints[:, 0:NM * TOP * E], pattern=[[0, NM * TOP], [1, E]], base=0, channel_multiplier=0))
            stepped(pool.tensor_copy(expert_id[:, :, :].rearrange("p a e -> p (a e)"), ints[:, 0:NM * TOP * E]))
            stepped(pool.iota(ints[:, 0:NM * E], pattern=[[0, NM], [CAP, E]], base=0, channel_multiplier=0))
            stepped(pool.tensor_copy(expert_base[:, :, :].rearrange("p m e -> p (m e)"), ints[:, 0:NM * E]))
            for h in range(2):
                stepped(pool.iota(ints[h * CHUNK:(h + 1) * CHUNK, :],
                                  pattern=[[TOP * CHUNK, NC], [TOP * 2 * S, NM], [1, TOP]],
                                  base=TOP * h * S, channel_multiplier=TOP))
            pool.tensor_copy(dest_id[:, :, :, :].rearrange("p c m k -> p (c m k)"), ints[:, :])\
                .then_inc(const_ready, 1)

            def spread(c, q):
                if first(c):
                    pool.wait_ge(slots_blank, 16)
                pool.wait_ge(rows_ready, 2 * c + 2)
                pool.wait_ge(meta_ready, 2 * c + 2)
                pool.wait_ge(slot_ready, c + 1)
                settle(pool, "pool")
                for m in range(NM):
                    for k in range(TOP):
                        n = m * TOP + k
                        pool.indirect_dma_start(
                            slots, bass.IndirectOffsetOnAxis(ap=slot_i[:, q, n:n + 1], axis=0),
                            rows[:, q, m, k, :], None, bounds_check=E * CAP - 1, oob_is_err=False)\
                            .then_inc(rows_sent[q], 16)

            def chunk(c, q, pairs):
                pool.wait_ge(mv2_ready, 2 * c + 2)
                settle(pool, "pool")
                pool.tensor_scalar(var2[:, :], mv2[:, :, 1], EPS, None, ALU.add).then_inc(rstd2_step, 1)
                pool.tensor_scalar(minus_mean2[:, :], mv2[:, :, 0], -1.0, None, ALU.mult)
                pool.wait_ge(rstd2_step, c + 1)
                if not first(c):
                    pool.wait_ge(z_ready, 2 * c)
                pool.tensor_tensor(rstd2[:, :], var2[:, :], minus_half[:, 0:NM], ALU.pow).then_inc(rstd2_ready, 1)
                pool.wait_ge(rstd2_ready, c + 1)
                pool.tensor_tensor(shift2[:, :], minus_mean2[:, :], rstd2[:, :], ALU.mult).then_inc(shift2_ready, 1)
                if not first(c):
                    spread(c - 1, 1 - q)

            for c in range(NC):
                chunk(c, c % 2, c // 2)
            spread(NC - 1, (NC - 1) % 2)

            for q in range(2):
                pool.wait_ge(rows_sent[q], 16 * NM * TOP * (NC // 2))
            pool.wait_ge(overflow_ready, 1)
            flag = pool.value_load(overflow[0:1, 0:1], min_val=0, max_val=1)
            with pool.If(flag > 0):
                for n in range(T * TOP // CAP + 1):
                    lo, hi = n * CAP, min((n + 1) * CAP, T * TOP)
                    k = (hi - lo) // P
                    pool.dma_start(chosen[lo:hi, :].rearrange("(p j) d -> p j d", j=k), blank[:, 0:k, 0:P])\
                        .then_inc(cleared, 16)
                pool.wait_ge(cleared, 16 * (T * TOP // CAP + 1))
                for q in range(2):
                    pool.wait_ge(rows_stored[q], 16 * (NC // 2))
                pool.wait_ge(late_slots, 1)
                with pool.Fori(0, NC) as c:
                    pool.dma_start(again_rows[:, :, :, :].rearrange("p m k r -> p (m k r)"),
                                   rows_kept[bass.ds(c, 1)].rearrange("o p n -> (o p) n")).then_inc(again_loaded, 16)
                    pool.tensor_copy(again_i[:, :], one(slot_il, c)).then_inc(again_copied, 1)
                    pool.wait_ge(again_loaded, 16 * c + 16)
                    pool.wait_ge(again_copied, c + 1)
                    settle(pool, "pool")
                    for m in range(NM):
                        for k in range(TOP):
                            n = m * TOP + k
                            pool.indirect_dma_start(
                                slots, bass.IndirectOffsetOnAxis(ap=again_i[:, n:n + 1], axis=0),
                                again_rows[:, m, k, :], None, bounds_check=E * CAP - 1, oob_is_err=False)\
                                .then_inc(again_sent, 16)
                    pool.wait_ge(again_sent, 16 * NM * TOP * (c + 1))
                    settle(pool, "pool")
            pool.sem_inc(dispatched, 1)

            def send(e, q, pairs):
                for n, (lo, hi) in enumerate(DOWN):
                    pool.wait_ge(result_ready, 2 * e + n + 1)
                    settle(pool, "pool")
                    for j in range(lo, hi):
                        pool.indirect_dma_start(
                            chosen, bass.IndirectOffsetOnAxis(ap=dst[:, q, j:j + 1], axis=0),
                            result[:, q, j, :], None, bounds_check=T * TOP - 1, oob_is_err=False)\
                            .then_inc(result_sent[q], 16)

            by_expert(send)(pool, E)

        @block.scalar
        def _(act):
            act.preload_act_table(ACT.Silu)

            def turn_x(g, lo, hi):
                act.wait_ge(xT_in_psum, g + 1)
                act.copy(xnT_all[:, lo:hi, :].rearrange("p c t -> p (c t)"),
                         turned[:, g % 2, 0:(hi - lo) * CT]).then_inc(xT_ready, 1)

            def gate_up(c, q):
                act.wait_ge(s_ready, c + 1)
                for n in range(NF // 2):
                    act.wait_ge(g_ready, NF // 2 * c + n + 1)
                    act.activation(gated[:, 2 * n:2 * n + 2, :], gu[:, 0, 2 * n:2 * n + 2, :], ACT.Silu,
                                   scale=s_cur[:, q:q + 1]).then_inc(gated_ready, 1)

            def normalise(c, q, pairs):
                if pairs_before(c):
                    act.wait_ge(rows_sent[q], 16 * NM * TOP * pairs)
                    act.wait_ge(rows_stored[q], 16 * pairs)
                act.wait_ge(shift2_ready, c + 1)
                act.wait_ge(rstd2_ready, c + 1)
                settle(act, "act")
                for m in range(NM):
                    act.activation(rows[:, q, m, 0, 0:P], one(x1_all, c)[:, m, :], ACT.Identity,
                                   scale=rstd2[:, m:m + 1], bias=shift2[:, m:m + 1]).then_inc(z_ready, 1)

            def address(c, q):
                if first(c):
                    act.wait_ge(const_ready, 3)
                act.wait_ge(z_ready, 2 * c + 2)
                act.copy(rows[:, q, :, 1, 0:P], rows[:, q, :, 0, 0:P]).then_inc(rows_ready, 1)
                act.copy(rows[:, q, :, :, DEST], one(dest_id, c)).then_inc(rows_ready, 1)

            def turn_z(c):
                act.wait_ge(zT_in_psum, c + 1)
                act.copy(zT[:, :], zT_ps).then_inc(zT_ready, 1)

            def weigh(c, q):
                act.wait_ge(gap_ready, c + 1)
                act.activation(half_tanh[:, :], gap[:, :], ACT.Tanh, scale=0.5).then_inc(tanh_ready, 1)
                act.wait_ge(tanh_ready, c + 1)
                for k, sign in enumerate((0.5, -0.5)):
                    act.activation(rows[:, q, :, k, GATE], half_tanh[:, :], ACT.Copy, scale=sign, bias=0.5)\
                        .then_inc(meta_ready, 1)

            def square(c):
                act.wait_ge(diff_ready, c + 1)
                act.activation(junk[:, :, :], diff[:, :, :], ACT.Square, accum_out=sq_sum[:, :]).then_inc(sq_ready, 1)

            def chunk(c, q, pairs):
                gate_up(c, q)
                if first(c):
                    turn_x(1, 1, 3)
                    act.wait_ge(shift1_ready, 1)
                    act.wait_ge(rstd1_ready, 3)
                    for t in range(SOON, NC * NM):
                        if t == SOON + 4:
                            square(0)
                        act.activation(xn_all[:, t // NM, t % NM, :], x_all[:, t // NM, t % NM, :], ACT.Identity,
                                       scale=rstd1[:, t:t + 1], bias=shift1[:, t:t + 1]).then_inc(xn_rest, 1)
                else:
                    normalise(c - 1, 1 - q, pairs - 1 + q)
                    turn_z(c - 1)
                    address(c - 1, 1 - q)
                    weigh(c - 1, 1 - q)
                    square(c)
                    if second(c):
                        turn_x(2, 3, 5)
                        turn_x(3, 5, 7)
                        turn_x(4, 7, 8)

            turn_x(0, 0, 1)
            for c in range(NC):
                chunk(c, c % 2, c // 2)
            normalise(NC - 1, (NC - 1) % 2, NC // 2 - 1)
            turn_z(NC - 1)
            address(NC - 1, (NC - 1) % 2)
            weigh(NC - 1, (NC - 1) % 2)
            act.preload_act_table(ACT.Gelu)
            act.wait_ge(b1_in_psum, 1)
            act.copy(b1T[:, :], b1T_ps).then_inc(b1_ready, 1)
            act.wait_ge(b1_ready, 1)

            def experts(e, q, pairs):
                for n, (lo, hi) in enumerate(HALVES):
                    for f in range(NEF):
                        act.wait_ge(hid_in_psum, 4 * e + 2 * n + f + 1)
                        settle(act, "act")
                        act.activation(hidden[:, f, lo:hi], hid_ps[:, 2 * n + f, 0:hi - lo], ACT.Gelu,
                                       bias=b1T[:, bass.ds(NEF * e + f, 1)]).then_inc(hid_ready, 1)

            by_expert(experts)(act, E)

        @block.vector
        def _(dve):
            dve.memset(s_cur[:, 0:1], 1.0).then_inc(s_ready, 1)
            dve.memset(s_sq[:, 0:1], 1.0).then_inc(s_sq_ready, 1)

            def norm1(lo, hi):
                for t in range(lo, hi):
                    dve.bn_stats(stats1[:, t, :], x_all[:, t // NM, t % NM, :]).then_inc(ln1_step, 1)
                for t in range(lo, hi):
                    dve.wait_ge(ln1_step, t + 1)
                    dve.bn_aggr(mv1[:, t, :], stats1[:, t, :]).then_inc(mv1_ready, 1)

            dve.wait_ge(x_first, 32)
            norm1(0, NM)
            dve.wait_ge(rstd1_ready, 1)
            dve.wait_ge(mv1_ready, NM)
            for m in range(NM):
                dve.tensor_scalar(xn_all[:, 0, m, :], x_all[:, 0, m, :], mv1[:, m, 0:1], rstd1[:, m:m + 1],
                                  ALU.subtract, ALU.mult).then_inc(xn_first, 1)

            def norm1_rest():
                dve.wait_ge(x_rest, 16 * B)
                norm1(NM, SOON)
                norm1(SOON, NC * NM)
                dve.wait_ge(rstd1_ready, 2)
                for t in range(NM, SOON):
                    dve.tensor_scalar(xn_all[:, t // NM, t % NM, :], x_all[:, t // NM, t % NM, :], mv1[:, t, 0:1],
                                      rstd1[:, t:t + 1], ALU.subtract, ALU.mult).then_inc(xn_soon, 1)
                dve.wait_ge(rstd1_ready, 3)
                dve.scalar_tensor_tensor(out=shift1[:, SOON:], in0=mv1[:, SOON:, 0], scalar=-1.0,
                                         in1=rstd1[:, SOON:], op0=ALU.mult, op1=ALU.mult).then_inc(shift1_ready, 1)

            def choose(c, q):
                dve.wait_ge(logits_in_psum, c + 1)
                settle(dve, "dve")
                for m in range(NM):
                    dve.max(best[:, m, :], logits_ps[:, m, :]).then_inc(best_ready, 1)
                dve.wait_ge(best_ready, 2 * c + 2)
                if not first(c):
                    dve.wait_ge(tanh_ready, c)
                dve.tensor_tensor(gap[:, :], best[:, :, 0], best[:, :, 1], ALU.subtract).then_inc(gap_ready, 1)

            def index_of(c):
                dve.wait_ge(best_ready, 2 * c + 2)
                settle(dve, "dve")
                for m in range(NM):
                    dve.max_index(best_id[:, m, :], best[:, m, :], logits_ps[:, m, :]).then_inc(best_id_ready, 1)

            def pick_of(c):
                dve.wait_ge(best_id_ready, 2 * c + 2)
                pick = one(pick_all, c)
                if first(c):
                    dve.wait_ge(const_ready, 3)
                dve.tensor_tensor(pick, expert_id[:, :, :].rearrange("p (m k) e -> p m k e", k=TOP),
                                  best_id[:, :, 0:TOP].rearrange("p m (k o) -> p m k o", o=1)
                                  .to_broadcast([P, NM, TOP, E]), ALU.is_equal).then_inc(pick_ready, 1)

            def mask_of(c):
                pick = one(pick_all, c)
                dve.wait_ge(pick_ready, c + 1)
                dve.tensor_tensor(one(mask_all, c), pick[:, :, 0, :], pick[:, :, 1, :], ALU.add)\
                    .then_inc(mask_ready, 1)

            def count_picks(c):
                dve.wait_ge(mask_ready, c + 1)
                if not first(c):
                    dve.wait_ge(before_ready, c)
                dve.tensor_tensor(one(before_all, c + 1), one(before_all, c), one(mask_all, c), ALU.add)\
                    .then_inc(before_ready, 1)

            def place(c, q):
                s = 4 * c
                dve.wait_ge(pos_ready, c + 1)
                dve.scalar_tensor_tensor(out=over[:, :, :], in0=pos_ps, scalar=CAP - 0.5, in1=nowhere[:, 0:NM, :],
                                         op0=ALU.is_gt, op1=ALU.mult).then_inc(slot_step, 1)
                dve.tensor_tensor(based[:, :, :], pos_ps, expert_base[:, :, :], ALU.add).then_inc(slot_step, 1)
                dve.wait_ge(slot_step, s + 2)
                dve.tensor_tensor(slot_of[:, :, :], over[:, :, :], based[:, :, :], ALU.add).then_inc(slot_step, 1)
                dve.wait_ge(slot_step, s + 3)
                for k in range(TOP):
                    dve.tensor_tensor(slot_pick[:, :, k, :], one(pick_all, c)[:, :, k, :], slot_of[:, :, :], ALU.mult)\
                        .then_inc(slot_picked, 1)
                dve.wait_ge(slot_picked, 2 * c + 2)
                dve.tensor_reduce(slot_f[:, :], slot_pick[:, :, :, :].rearrange("p m k e -> p (m k) e"), AX.X, ALU.add)\
                    .then_inc(slot_step, 1)
                dve.wait_ge(slot_step, s + 4)
                dve.tensor_copy(slot_i[:, q, :], slot_f[:, :]).then_inc(slot_ready, 1)

            def chunk(c, q, pairs):
                for n in range(NF // 2):
                    dve.wait_ge(u_ready, NF // 2 * c + n + 1)
                    dve.wait_ge(gated_ready, NF // 2 * c + n + 1)
                    dve.tensor_tensor(prod[:, 2 * n:2 * n + 2, :], gated[:, 2 * n:2 * n + 2, :],
                                      gu[:, 1, 2 * n:2 * n + 2, :], ALU.mult).then_inc(prod_ready, 1)
                if pairs_before(c):
                    place(c - 2, q)
                if first(c):
                    norm1_rest()
                if not first(c):
                    choose(c - 1, 1 - q)
                dve.wait_ge(out_ready, c + 1)
                dve.wait_ge(s_sq_ready, c + 1)
                if first(c):
                    dve.wait_ge(xn_first, NM)
                if second(c):
                    dve.wait_ge(xn_soon, SOON - NM)
                    dve.wait_ge(xn_rest, NC * NM - SOON)
                o = out_ps
                dve.scalar_tensor_tensor(out=diff[:, :, :], in0=o, scalar=s_sq[:, q:q + 1], in1=one(xn_all, c),
                                         op0=ALU.mult, op1=ALU.subtract).then_inc(diff_ready, 1)
                if not first(c):
                    index_of(c - 1)
                dve.scalar_tensor_tensor(out=one(x1_all, c), in0=o, scalar=s_sq[:, q:q + 1], in1=one(x_all, c),
                                         op0=ALU.mult, op1=ALU.add).then_inc(x1_ready, 1)
                if not first(c):
                    pick_of(c - 1)
                dve.wait_ge(x1_ready, c + 1)
                settle(dve, "dve")
                for m in range(NM):
                    if m == 1:
                        dve.wait_ge(loss_ready, c + 1)
                        dve.scalar_tensor_tensor(out=s_cur[:, 1 - q:2 - q], in0=loss_ps, scalar=1.0,
                                                 in1=s_cur[:, q:q + 1], op0=ALU.add, op1=ALU.mult).then_inc(s_ready, 1)
                        settle(dve, "dve")
                    dve.bn_stats(stats2[:, m, :], one(x1_all, c)[:, m, :]).then_inc(stats2_done, 1)
                if not first(c):
                    mask_of(c - 1)
                dve.wait_ge(stats2_done, 2 * c + 2)
                settle(dve, "dve")
                if not first(c):
                    dve.wait_ge(shift2_ready, c)
                    settle(dve, "dve")
                for m in range(NM):
                    dve.bn_aggr(mv2[:, m, :], stats2[:, m, :]).then_inc(mv2_ready, 1)
                if not first(c):
                    count_picks(c - 1)
                dve.wait_ge(s_ready, c + 2)
                dve.tensor_tensor(s_sq[:, 1 - q:2 - q], s_cur[:, 1 - q:2 - q], s_cur[:, 1 - q:2 - q], ALU.mult)\
                    .then_inc(s_sq_ready, 1)

            for c in range(NC):
                chunk(c, c % 2, c // 2)
            place(NC - 2, (NC - 2) % 2)
            choose(NC - 1, (NC - 1) % 2)
            index_of(NC - 1)
            pick_of(NC - 1)
            mask_of(NC - 1)
            count_picks(NC - 1)
            place(NC - 1, (NC - 1) % 2)

            dve.wait_ge(count_ready, 1)
            dve.tensor_reduce(most[:, :], count_ps, AX.X, ALU.max).then_inc(most_ready, 1)
            dve.wait_ge(most_ready, 1)
            dve.tensor_scalar(overflow[:, :], most[:, :], CAP + 0.5, None, ALU.is_gt).then_inc(overflow_ready, 1)

            dve.wait_ge(before_ready, NC)
            total = before_all[:, NC:NC + 1].to_broadcast([P, NC, NM, E])
            dve.tensor_tensor(after_all[:, :, :, :], total, before_all[:, 0:NC], ALU.subtract).then_inc(after_step, 1)
            dve.wait_ge(after_step, 1)
            dve.tensor_tensor(after_all[:, :, :, :], after_all[:, :, :, :], mask_all[:, :, :, :], ALU.subtract)\
                .then_inc(after_ready, 1)
            dve.wait_ge(rank_ready, 1)
            ranks = rank_ps.rearrange("p c m e -> p (c m) e")
            dve.scalar_tensor_tensor(out=over_l[:, :, :], in0=ranks, scalar=CAP - 0.5, in1=nowhere[:, :, :],
                                     op0=ALU.is_gt, op1=ALU.mult).then_inc(late_step, 1)
            dve.tensor_tensor(based_l[:, :, :], ranks, expert_base[:, 0:1, :].to_broadcast([P, NC * NM, E]), ALU.add)\
                .then_inc(late_step, 1)
            dve.wait_ge(late_step, 2)
            dve.tensor_tensor(over_l[:, :, :], over_l[:, :, :], based_l[:, :, :], ALU.add).then_inc(late_step, 1)
            dve.wait_ge(late_step, 3)
            for k in range(TOP):
                dve.tensor_tensor(pick_l[:, :, k, :], pick_all[:, :, :, k, :].rearrange("p c m e -> p (c m) e"),
                                  over_l[:, :, :], ALU.mult).then_inc(late_step, 1)
            dve.wait_ge(late_step, 5)
            dve.tensor_reduce(slot_fl[:, :], pick_l[:, :, :, :].rearrange("p a k e -> p (a k) e"), AX.X, ALU.add)\
                .then_inc(late_step, 1)
            dve.wait_ge(late_step, 6)
            dve.tensor_copy(slot_il[:, :, :].rearrange("p c n -> p (c n)"), slot_fl[:, :]).then_inc(late_slots, 1)

            def take_slots(e):
                dve.wait_ge(xsT_in_psum, e + 1)
                dve.tensor_copy(xsT[:, :], xsT_ps).then_inc(xsT_ready, 1)

            def expert(e, q, pairs):
                if not (isinstance(e, int) and e == E - 1):
                    take_slots(e + 1)
                dve.wait_ge(xs_loaded[q], 16 * pairs + 16)
                if pairs_before(e):
                    dve.wait_ge(result_sent[q], 16 * NJ * pairs)
                dve.tensor_copy(dst[:, q, :], xs[:, q, :, DEST]).then_inc(xs_read, 1)
                dve.tensor_copy(wgt[:, q, :], xs[:, q, :, GATE]).then_inc(xs_read, 1)
                dve.wait_ge(xs_read, 2 * e + 2)
                for n, (lo, hi) in enumerate(DOWN):
                    dve.wait_ge(eo_in_psum, 2 * e + n + 1)
                    dve.tensor_tensor(biased[:, lo:hi, :], eo_ps[:, n, 0:hi - lo, :],
                                      b2_sb[:, bass.ds(e, 1)].to_broadcast([P, hi - lo, P]), ALU.add)\
                        .then_inc(biased_ready, 1)
                    dve.wait_ge(biased_ready, 2 * e + n + 1)
                    dve.tensor_tensor(result[:, q, lo:hi, :], biased[:, lo:hi, :],
                                      wgt[:, q, lo:hi].rearrange("p (j o) -> p j o", o=1).to_broadcast([P, hi - lo, P]),
                                      ALU.mult).then_inc(result_ready, 1)

            dve.wait_ge(b_exp, 32)
            take_slots(0)
            by_expert_ahead(expert)(dve, E)

            for n, (m, lo, hi) in enumerate(PIECES):
                dve.wait_ge(picked_loaded[n], 32)
                dve.tensor_tensor(summed[:, m, lo:hi], picked[:, m, lo:hi, 0:P], picked[:, m, lo:hi, P:2 * P], ALU.add)\
                    .then_inc(summed_ready, 1)
                dve.wait_ge(summed_ready, n + 1)
                dve.tensor_tensor(final[:, m, lo:hi], summed[:, m, lo:hi], x1_all[:, lo:hi, m, :], ALU.add)\
                    .then_inc(final_ready, 1)

        @block.tensor
        def _(pe):
            pe.wait_ge(const_ready, 1)

            def turn_x(g, lo, hi):
                if g == 0:
                    pe.wait_ge(xn_first, NM)
                elif g == 1:
                    pe.wait_ge(xn_soon, SOON - NM)
                else:
                    pe.wait_ge(xn_rest, NM * hi - SOON)
                    pe.wait_ge(xT_ready, g - 1)
                if g == 2:
                    pe.wait_ge(zT_ready, 1)
                if g == 3:
                    pe.wait_ge(s_ready, 2)
                for n in range(NM * (hi - lo)):
                    t = pe.transpose(turned[:, g % 2, n * P:(n + 1) * P], xn_all[:, lo + n // NM, n % NM, :], ident[:, :])
                t.then_inc(xT_in_psum, 1)

            def up(c, a, n):
                for f in (2 * n, 2 * n + 1):
                    mm = pe.matmul(gu[:, a, f, :], (w0_sb, w2_sb)[a][:, f * P:(f + 1) * P], one2(xnT_all, c),
                                   start=True, stop=True)
                    if (a, n, f) == (0, 1, 2) and not first(c):
                        loss(c - 1)
                mm.then_inc((g_ready, u_ready)[a], 1)

            def one2(ap, i):
                return ap[:, bass.ds(i, 1)].rearrange("p o t -> p (o t)")

            def down(c, q):
                for m in range(NM):
                    for f in range(NF):
                        if m == 0 and f % 2 == 0:
                            pe.wait_ge(prod_ready, NF // 2 * c + f // 2 + 1)
                        mm = pe.matmul(out_ps[:, m, :], prod[:, f, m * P:(m + 1) * P], w1_sb[:, f, :],
                                       start=(f == 0), stop=(f == NF - 1))
                        if m == 1 and f == NF // 2 - 1 and not first(c):
                            route(c - 1)
                    if m == 0 and not first(c):
                        turn_z(c - 1, 1 - q)
                mm.then_inc(out_ready, 1)

            def loss(c):
                pe.wait_ge(sq_ready, c + 1)
                pe.matmul(loss_ps, loss_w[:, :], sq_sum[:, :], start=True, stop=True).then_inc(loss_ready, 1)

            def turn_z(c, q):
                pe.wait_ge(z_ready, 2 * c + 2)
                for m in range(NM):
                    t = pe.transpose(zT_ps[:, m * P:(m + 1) * P], rows[:, q, m, 0, 0:P], ident[:, :])
                t.then_inc(zT_in_psum, 1)

            def route(c):
                if not first(c):
                    pe.wait_ge(slot_step, 4 * c)
                pe.matmul(logits_ps, ones_row[:, :], rb_sb[:, :].rearrange("p (o e) -> p o e", o=1)
                          .to_broadcast([1, NM, E]), start=True, stop=False)
                pe.wait_ge(zT_ready, c + 1)
                for m in range(NM):
                    mm = pe.matmul(logits_ps[:, m, :], zT[:, m * P:(m + 1) * P], rw_sb[:, :],
                                   start=False, stop=(m == NM - 1))
                mm.then_inc(logits_in_psum, 1)

            def position(c):
                pe.wait_ge(mask_ready, c + 1)
                if not first(c):
                    pe.wait_ge(before_ready, c)
                mask, before = one(mask_all, c), one(before_all, c)
                pe.matmul(pos_ps, earlier[:, :], mask, start=True, stop=False)
                for m in range(NM):
                    pe.matmul(pos_ps, ones[:, :], before[:, m:m + 1, :].to_broadcast([P, NM, E]),
                              start=False, stop=False)
                pe.matmul(pos_ps[:, 1, :], ones[:, :], mask[:, 0, :], start=False, stop=True)\
                    .then_inc(pos_ready, 1)

            def chunk(c, q, pairs):
                up(c, 1, 0)
                up(c, 0, 1)
                up(c, 1, 1)
                if pairs_before(c):
                    position(c - 2)
                if first(c):
                    pe.wait_ge(w_down, 16)
                    down(c, q)
                    turn_x(1, 1, 3)
                    pe.wait_ge(xT_ready, 2)
                if not (isinstance(c, int) and c == NC - 1):
                    pe.wait_ge(gated_ready, NF // 2 * c + 1)
                    up(c + 1, 0, 0)
                if not first(c):
                    if second(c):
                        pe.wait_ge(w_route, 32)
                    pe.wait_ge(x1_ready, c)
                    down(c, q)
                if second(c):
                    turn_x(2, 3, 5)
                    turn_x(3, 5, 7)
                    turn_x(4, 7, 8)
                    pe.wait_ge(xT_ready, 5)

            turn_x(0, 0, 1)
            pe.wait_ge(xT_ready, 1)
            pe.wait_ge(w_up, 32)
            up(0, 0, 0)
            for c in range(NC):
                chunk(c, c % 2, c // 2)
            loss(NC - 1)
            position(NC - 2)
            turn_z(NC - 1, (NC - 1) % 2)
            route(NC - 1)
            pe.wait_ge(b_exp, 32)
            pe.transpose(b1T_ps, b1_rows[:, :], ident[0:E * NEF, 0:E * NEF]).then_inc(b1_in_psum, 1)
            position(NC - 1)

            pe.wait_ge(before_ready, NC)
            for m in range(NM):
                mm = pe.matmul(count_ps, ones[:, :], before_all[:, NC, m, :], start=(m == 0), stop=(m == NM - 1))
            mm.then_inc(count_ready, 1)
            pe.matmul(rank_ps, earlier[:, :], mask_all[:, :, :, :], start=True, stop=False)
            pe.matmul(rank_ps, same_or_earlier_row[:, :], before_all[:, 0:NC], start=False, stop=False)
            pe.wait_ge(after_ready, 1)
            pe.matmul(rank_ps, earlier_row[:, :], after_all[:, :, :, :], start=False, stop=False)
            pe.matmul(rank_ps[:, :, 1, :], ones[:, :], before_all[:, NC, 0:1, :].to_broadcast([P, NC, E]),
                      start=False, stop=True).then_inc(rank_ready, 1)

            def turn_slots(e, q, pairs):
                pe.wait_ge(xs_loaded[q], 16 * pairs + 16)
                if first(e):
                    pe.wait_ge(late_slots, 1)
                    pe.wait_ge(overflow_ready, 1)
                    pe.wait_ge(b1_ready, 1)
                for j in range(NJ):
                    t = pe.transpose(xsT_ps[:, j * P:(j + 1) * P], xs[:, q, j, 0:P], ident[:, :])
                t.then_inc(xsT_in_psum, 1)

            def expert(e, q, pairs):
                pe.wait_ge(xsT_ready, e + 1)
                pe.wait_ge(we_loaded[q], 32 * pairs + 32)
                for n, (lo, hi) in enumerate(HALVES):
                    for f in range(NEF):
                        pe.matmul(hid_ps[:, 2 * n + f, 0:hi - lo], we1_sb[:, q, f * P:(f + 1) * P], xsT[:, lo:hi],
                                  start=True, stop=True).then_inc(hid_in_psum, 1)
                nxt = (e + 1, 1 - q, pairs + q)
                if not (isinstance(e, int) and e == E - 1):
                    turn_slots(*nxt)
                for n, (lo, hi) in enumerate(DOWN):
                    pe.wait_ge(hid_ready, 4 * e + 2 * n + 2)
                    if n == 0 and not first(e):
                        pe.wait_ge(biased_ready, 2 * e)
                    for j in range(lo, hi):
                        for f in range(NEF):
                            mm = pe.matmul(eo_ps[:, n, j - lo, :], hidden[:, f, j * P:(j + 1) * P], we2_sb[:, q, f, :],
                                           start=(f == 0), stop=(f == NEF - 1))
                    mm.then_inc(eo_in_psum, 1)

            turn_slots(0, 0, 0)
            by_expert_ahead(expert)(pe, E)


_INS = ['L0_attn_x', 'L0_attn_w0', 'L0_attn_w1', 'L0_attn_w2', 'L0_ffn_router_w', 'L0_ffn_router_b',
        'L0_ffn_w1', 'L0_ffn_b1', 'L0_ffn_w2', 'L0_ffn_b2']
_OUTS = [((4, 512, 128), 'float32')]


def kernel(**inputs):
    import numpy as _np
    import concourse.bacc as _bacc
    from concourse import mybir as _mybir
    from concourse.bass_utils import run_bass_kernel_spmd as _run

    nc = _bacc.Bacc("TRN2", target_bir_lowering=False, num_devices=1)
    arrays, args = {}, []
    for name in _INS:
        a = _np.ascontiguousarray(inputs[name])
        arrays[f"in_{name}_dram"] = a
        args.append(nc.dram_tensor(f"in_{name}_dram", a.shape, _mybir.dt.from_np(a.dtype), kind="ExternalInput").ap())
    for i, (shape, dtype) in enumerate(_OUTS):
        dt = _mybir.dt.from_np(_np.dtype(dtype))
        args.append(nc.dram_tensor(f"out_{i}_dram", shape, dt, kind="ExternalOutput").ap())
    block_kernel(nc, *args)
    r = _run(nc, [arrays], core_ids=[0])
    got = tuple(r.results[0][f"out_{i}_dram"] for i in range(len(_OUTS)))
    return got[0]
```

```python
from contextlib import ExitStack

import concourse.bass as bass
from concourse import mybir

ALU = mybir.AluOpType
ACT = mybir.ActivationFunctionType
AX = mybir.AxisListType
F32 = mybir.dt.float32
F32R = mybir.dt.float32r
BF16 = mybir.dt.bfloat16
I32 = mybir.dt.int32
U32 = mybir.dt.uint32

P = 128
CHUNK = 64
LR = 0.001
EPS = 1e-5
TOP = 2
ROW = P + 4
DEST, GATE = P, P + 1
SPLIT = 3
NOWHERE = 1.0e6


def block_kernel(nc, x, w0, w1, w2, router_w, router_b, we1, be1, we2, be2, out):
    B, S, D = x.shape
    F = w0.shape[1]
    E = router_w.shape[1]
    EF = we1.shape[2]
    NC = S // CHUNK
    NM = B * CHUNK // P
    CT = NM * P
    NF = F // P
    NEF = EF // P
    T = B * S
    CAP = -(-5 * T * TOP // (4 * E))
    NJ = CAP // P
    NR = 4
    assert D == P and NM == 2 and CAP % P == 0 and NC % NR == 0 and E == 8
    NORMS = (0, 1, 3, 5, NC)
    BY_ACT = 4
    HALVES = ((0, 2 * P), (2 * P, CAP))
    DOWN = ((0, 2), (2, NJ))
    PIECES = [(0, 0, NC // 2), (0, NC // 2, NC), (1, 0, NC // 2 + 1), (1, NC // 2 + 1, NC)]

    slots = nc.dram_tensor("slots", [E * CAP, ROW], F32).ap()
    rows_kept = nc.dram_tensor("rows_kept", [NC, P, NM * TOP * ROW], F32).ap()
    chosen = nc.dram_tensor("chosen", [T * TOP, P], F32).ap()

    with ExitStack() as ctx:
        def sb(name, shape, dt=F32):
            return ctx.enter_context(nc.sbuf_tensor(name, shape, dt))

        def ps(name, shape):
            return ctx.enter_context(nc.psum_tensor(name, shape, F32))

        def sem(name):
            return ctx.enter_context(nc.semaphore(name))

        ident = sb("ident", [P, P])
        earlier = sb("earlier", [P, P], BF16)
        same_or_earlier_row = sb("same_or_earlier_row", [P, P], BF16)
        earlier_row = sb("earlier_row", [P, P], BF16)
        ones = sb("ones", [P, P], BF16)
        warm = sb("warm", [P, 512], BF16)
        loss_w = sb("loss_w", [P, P])
        expert_id = sb("expert_id", [P, NM * TOP, E])
        expert_base = sb("expert_base", [P, NM, E])
        nowhere = sb("nowhere", [P, NC * NM, E])
        dest_id = sb("dest_id", [P, NC, NM, TOP])
        minus_half = sb("minus_half", [P, NC * NM])
        blank = sb("blank", [P, NJ, ROW])
        ints = sb("ints", [P, NC * NM * TOP], I32)
        w0_sb = sb("w0_sb", [P, F])
        w2_sb = sb("w2_sb", [P, F])
        w1_sb = sb("w1_sb", [P, NF, P])
        rw_sb = sb("rw_sb", [P, E])
        rb_sb = sb("rb_sb", [SPLIT, E])
        rb_high = sb("rb_high", [SPLIT, SPLIT, E], BF16)
        rb_left = sb("rb_left", [SPLIT, SPLIT, E])
        rb_part = sb("rb_part", [SPLIT, SPLIT, E])
        rb_sum = sb("rb_sum", [SPLIT, E])
        rb_split = sb("rb_split", [SPLIT, E], BF16)
        x_all = sb("x_all", [P, NC, NM, P])
        xn_all = sb("xn_all", [P, NC, NM, P])
        xnT_first = sb("xnT_first", [P, CT])
        xnT_high = sb("xnT_high", [P, NC, CT], F32R)
        xnT_rest = sb("xnT_rest", [P, NC, CT], F32R)
        w_high = sb("w_high", [P, 2, F], F32R)
        w_rest = sb("w_rest", [P, 2, F], F32R)
        x1_all = sb("x1_all", [P, NC, NM, P])
        stats1 = sb("stats1", [P, NC * NM, 6])
        mv1 = sb("mv1", [P, NC * NM, 2])
        var1 = sb("var1", [P, NC * NM])
        rstd1 = sb("rstd1", [P, NC * NM])
        shift1 = sb("shift1", [P, NC * NM])
        gated = sb("gated", [P, NF, CT])
        prod = sb("prod", [P, NF, CT])
        s_cur = sb("s_cur", [P, 2])
        s_sq = sb("s_sq", [P, 2])
        diff = sb("diff", [P, NM, P])
        junk = sb("junk", [P, NM, P])
        sq_sum = sb("sq_sum", [P, 1])
        stats2 = sb("stats2", [P, NM, 6])
        mv2 = sb("mv2", [P, NM, 2])
        var2 = sb("var2", [P, NM])
        rstd2 = sb("rstd2", [P, NM])
        shift2 = sb("shift2", [P, NM])
        minus_mean2 = sb("minus_mean2", [P, NM])
        rows = sb("rows", [P, NR, NM, TOP, ROW])
        zT = sb("zT", [P, CT])
        best = sb("best", [P, NM, 8])
        best_id = sb("best_id", [P, NM, 8], U32)
        gap = sb("gap", [P, NM])
        half_tanh = sb("half_tanh", [P, NM])
        pick_all = sb("pick_all", [P, NC, NM, TOP, E])
        mask_all = sb("mask_all", [P, NC, NM, E], BF16)
        before_all = sb("before_all", [P, NC + 1, NM, E], BF16)
        after_all = sb("after_all", [P, NC, NM, E], BF16)
        over = sb("over", [P, NM, E])
        based = sb("based", [P, NM, E])
        slot_of = sb("slot_of", [P, NM, E])
        slot_pick = sb("slot_pick", [P, NM, TOP, E])
        slot_f = sb("slot_f", [P, NM * TOP])
        slot_i = sb("slot_i", [P, NC, NM * TOP], I32)
        most = sb("most", [P, 1])
        overflow = sb("overflow", [P, 1], I32)
        over_l = sb("over_l", [P, NC * NM, E])
        based_l = sb("based_l", [P, NC * NM, E])
        pick_l = sb("pick_l", [P, NC * NM, TOP, E])
        slot_fl = sb("slot_fl", [P, NC * NM * TOP])
        slot_il = sb("slot_il", [P, NC, NM * TOP], I32)
        again_i = sb("again_i", [P, NM * TOP], I32)
        again_rows = sb("again_rows", [P, NM, TOP, ROW])
        b1_rows = sb("b1_rows", [E * NEF, P])
        b1T = sb("b1T", [P, E * NEF])
        b2_sb = sb("b2_sb", [P, E, P])
        we1_sb = sb("we1_sb", [P, 2, EF])
        we2_sb = sb("we2_sb", [P, 2, NEF, P])
        xs = sb("xs", [P, 2, NJ, ROW])
        xsT = sb("xsT", [P, CAP])
        hidden = sb("hidden", [P, NEF, CAP])
        dst = sb("dst", [P, 2, NJ], I32)
        wgt = sb("wgt", [P, 2, NJ])
        biased = sb("biased", [P, NJ, P])
        result = sb("result", [P, 2, NJ, P])
        picked = sb("picked", [P, NM, NC, TOP * P])
        summed = sb("summed", [P, NM, NC, P])
        final = sb("final", [P, NM, NC, P])

        gu = ps("gu", [P, 2, NF, CT])
        turned = ps("turned", [P, 2, 512])
        outp = ps("outp", [P, 2, 512])
        zT_ps = turned[:, 0, 0:CT]

        def xT_ps(c):
            return turned[:, 1 if c == 1 else 0, 0:CT]

        loss_ps = turned[:, 1, 0:1]
        b1T_ps = turned[:, 0, 0:E * NEF]
        count_ps = turned[:, 1, 0:E]
        out_ps = outp[:, 0, 0:NM * P].rearrange("p (m d) -> p m d", d=P)
        logits_ps = outp[:, 1, 0:NM * E].rearrange("p (m e) -> p m e", e=E)
        pos_ps = outp[:, 1, 32:32 + NM * E].rearrange("p (m e) -> p m e", e=E)
        rank_ps = outp[:, 0, 0:NC * NM * E].rearrange("p (c m e) -> p c m e", m=NM, e=E)
        hid_ps = gu[:, :, :, :].rearrange("p a f t -> p (a f t)").rearrange("p (b n) -> p b n", n=512)
        xsT_ps = turned
        eo_ps = outp[:, :, :].rearrange("p a (j d) -> p a j d", d=P)

        x_first, x_soon, x_rest, w_up, w_down, w_route, b_exp = (sem(n) for n in (
            "x_first", "x_soon", "x_rest", "w_up", "w_down", "w_route", "b_exp"))
        blank_made, slots_blank = sem("blank_made"), sem("slots_blank")
        const_step, const_ready = sem("const_step"), sem("const_ready")
        ln1_step, mv1_ready, rstd1_step = sem("ln1_step"), sem("mv1_ready"), sem("rstd1_step")
        rstd1_ready, xn_first, xn_rest = sem("rstd1_ready"), sem("xn_first"), sem("xn_rest")
        shift1_ready = sem("shift1_ready")
        xT_in_psum, xT_first, xT_high, xT_ready = (sem(n) for n in ("xT_in_psum", "xT_first", "xT_high", "xT_ready"))
        warm_ready, bias_ready = sem("warm_ready"), sem("bias_ready")
        w_high_ready, w_ready = sem("w_high_ready"), sem("w_ready")
        b1_in_psum, b1_ready = sem("b1_in_psum"), sem("b1_ready")
        g_ready, u_ready, gated_ready, prod_ready = (sem(n) for n in (
            "g_ready", "u_ready", "gated_ready", "prod_ready"))
        out_ready, diff_ready, x1_ready = sem("out_ready"), sem("diff_ready"), sem("x1_ready")
        sq_ready, loss_ready, s_ready, s_sq_ready = (sem(n) for n in (
            "sq_ready", "loss_ready", "s_ready", "s_sq_ready"))
        minus_mean2_ready, z_last = sem("minus_mean2_ready"), sem("z_last")
        stats2_done, mv2_ready, rstd2_step, rstd2_ready = (sem(n) for n in (
            "stats2_done", "mv2_ready", "rstd2_step", "rstd2_ready"))
        shift2_ready, z_ready, rows_ready, zT_in_psum, zT_ready, logits_in_psum = (sem(n) for n in (
            "shift2_ready", "z_ready", "rows_ready", "zT_in_psum", "zT_ready", "logits_in_psum"))
        best_ready, best_id_ready, gap_ready, tanh_ready, pick_ready, mask_ready = (sem(n) for n in (
            "best_ready", "best_id_ready", "gap_ready", "tanh_ready", "pick_ready", "mask_ready"))
        pos_ready, slot_step, slot_picked, slot_ready, before_ready, meta_ready = (sem(n) for n in (
            "pos_ready", "slot_step", "slot_picked", "slot_ready", "before_ready", "meta_ready"))
        rows_stored = [sem(f"rows_stored{r}") for r in range(NR)]
        rows_sent = [sem(f"rows_sent{r}") for r in range(NR)]
        count_ready, most_ready, overflow_ready = sem("count_ready"), sem("most_ready"), sem("overflow_ready")
        after_step, after_ready, rank_ready = sem("after_step"), sem("after_ready"), sem("rank_ready")
        late_step, late_slots = sem("late_step"), sem("late_slots")
        cleared, again_loaded, again_copied, again_sent = (sem(n) for n in (
            "cleared", "again_loaded", "again_copied", "again_sent"))
        dispatched = sem("dispatched")
        settled = {k: sem(f"settled_{k}") for k in ("pool", "act")}
        xs_loaded = [sem(f"xs_loaded{q}") for q in range(2)]
        we_loaded = [sem(f"we_loaded{q}") for q in range(2)]
        xs_begun = sem("xs_begun")
        xs_read, xsT_in_psum, xsT_ready = sem("xs_read"), sem("xsT_in_psum"), sem("xsT_ready")
        hid_in_psum, hid_ready, eo_in_psum = sem("hid_in_psum"), sem("hid_ready"), sem("eo_in_psum")
        biased_ready, result_ready = sem("biased_ready"), sem("result_ready")
        result_sent = [sem(f"result_sent{q}") for q in range(2)]
        picked_loaded = [sem(f"picked_loaded{m}") for m in range(len(PIECES))]
        summed_ready, final_ready, out_stored = sem("summed_ready"), sem("final_ready"), sem("out_stored")

        def by_expert(step):
            def run(eng, n):
                step(0, 0, 0)
                step(1, 1, 0)
                with eng.Fori(0, n // 2 - 1) as i:
                    step(2 * i + 2, 0, i + 1)
                    step(2 * i + 3, 1, i + 1)
            return run

        def by_expert_ahead(step):
            def run(eng, n):
                step(0, 0, 0)
                step(1, 1, 0)
                with eng.Fori(0, n // 2 - 2) as i:
                    step(2 * i + 2, 0, i + 1)
                    step(2 * i + 3, 1, i + 1)
                step(n - 2, 0, n // 2 - 1)
                step(n - 1, 1, n // 2 - 1)
            return run

        def first(e):
            return isinstance(e, int) and e == 0

        def last_expert(e):
            return isinstance(e, int) and e == E - 1

        def pairs_before(e):
            return not (isinstance(e, int) and e < 2)

        def settle(eng, who):
            eng.sem_inc(settled[who], 1)

        block = ctx.enter_context(nc.Block())

        @block.sync
        def _(sp):
            def token_rows(t, b):
                return t[b].rearrange("(c s) d -> s c d", s=CHUNK)

            for h in range(2):
                part = slice(h * CHUNK, (h + 1) * CHUNK)
                sp.dma_start(x_all[part, 0, :, :],
                             x[h::2, 0:CHUNK, :].rearrange("m s d -> s m d")).then_inc(x_first, 16)
            sp.dma_start(w0_sb[:, :], w0).then_inc(w_up, 16)
            sp.dma_start(w2_sb[:, :], w2).then_inc(w_up, 16)

            def load_x(lo, hi, signal):
                for b in range(B):
                    part = slice((b % 2) * CHUNK, (b % 2 + 1) * CHUNK)
                    sp.dma_start(x_all[part, lo:hi, b // 2, :], token_rows(x, b)[:, lo:hi, :]).then_inc(signal, 16)

            load_x(1, 3, x_soon)
            sp.dma_start(w1_sb[:, :, :], w1.rearrange("(f p) d -> p f d", p=P)).then_inc(w_down, 16)
            load_x(3, NC, x_rest)
            sp.dma_start(rw_sb[:, :], router_w).then_inc(w_route, 16)
            sp.dma_start(rb_sb[:, :], router_b.rearrange("(o e) -> o e", o=1).to_broadcast([SPLIT, E]))\
                .then_inc(w_route, 16)
            sp.dma_start(b1_rows[:, :], be1.rearrange("e (f p) -> (e f) p", p=P)).then_inc(b_exp, 16)
            sp.wait_ge(blank_made, 2)
            sp.dma_start(slots.rearrange("(e p j) r -> p e (j r)", p=P, j=NJ),
                         blank[:, :, :].rearrange("p (o j) r -> p o (j r)", o=1).to_broadcast([P, E, NJ * ROW]))\
                .then_inc(slots_blank, 16)
            sp.dma_start(b2_sb[:, :, :].rearrange("p e d -> p (e d)"),
                         be2.rearrange("(o e) d -> o (e d)", o=1).to_broadcast([P, E * D])).then_inc(b_exp, 16)

            def load_expert(e, q):
                sp.dma_start(we1_sb[:, q], we1[bass.ds(e, 1)].rearrange("o d f -> (o d) f")).then_inc(we_loaded[q], 16)
                sp.dma_start(we2_sb[:, q], we2[bass.ds(e, 1)].rearrange("o (f p) d -> p (o f) d", p=P))\
                    .then_inc(we_loaded[q], 16)

            load_expert(0, 0)
            load_expert(1, 1)

            for c in range(NC):
                sp.wait_ge(rows_ready, 2 * c + 2)
                sp.wait_ge(meta_ready, 2 * c + 2)
                sp.dma_start(rows_kept[c], rows[:, c % NR].rearrange("p m k r -> p (m k r)"))\
                    .then_inc(rows_stored[c % NR], 16)

            sp.wait_ge(dispatched, 1)
            for r in range(NR):
                sp.wait_ge(rows_sent[r], 16 * NM * TOP * (NC // NR))

            def load_slots(e, q, pairs):
                if not isinstance(e, int):
                    sp.wait_ge(xsT_in_psum, 2 * e - 2)
                    sp.wait_ge(xs_read, 2 * e - 2)
                rows_of = slots[bass.ds(e * CAP, CAP), :].rearrange("(p j) r -> p j r", j=NJ)
                begin = 0
                if first(e):
                    begin = DOWN[0][1]
                    sp.dma_start(xs[:, q, 0:begin], rows_of[:, 0:begin, :]).then_inc(xs_begun, 16)
                sp.dma_start(xs[:, q, begin:NJ], rows_of[:, begin:NJ, :]).then_inc(xs_loaded[q], 16)
                if not isinstance(e, int):
                    sp.wait_ge(eo_in_psum, 2 * e - 2)
                    load_expert(e, q)

            by_expert(load_slots)(sp, E)

            for q in range(2):
                sp.wait_ge(result_sent[q], 16 * NJ * (E // 2))
            by_token = chosen.rearrange("(b c s k) d -> b s c (k d)", b=B, c=NC, k=TOP)
            for n, (m, lo, hi) in enumerate(PIECES):
                for h in range(2):
                    sp.dma_start(picked[h * CHUNK:(h + 1) * CHUNK, m, lo:hi, :], by_token[2 * m + h][:, lo:hi, :])\
                        .then_inc(picked_loaded[n], 16)
            for n, (m, lo, hi) in enumerate(PIECES):
                sp.wait_ge(final_ready, n + 1)
                for h in range(2):
                    sp.dma_start(token_rows(out, 2 * m + h)[:, lo:hi, :],
                                 final[h * CHUNK:(h + 1) * CHUNK, m, lo:hi, :]).then_inc(out_stored, 16)
            sp.wait_ge(out_stored, 32 * len(PIECES))

        @block.gpsimd
        def _(pool):
            pool.memset(blank[:, :, :], 0.0).then_inc(blank_made, 1)
            pool.wait_ge(blank_made, 1)
            pool.memset(blank[:, :, DEST:DEST + 1], NOWHERE).then_inc(blank_made, 1)
            pool.memset(minus_half[:, :], -0.5)
            pool.memset(ident[:, :], 0.0).then_inc(const_step, 1)
            pool.memset(earlier[:, :], 1.0).then_inc(const_step, 1)
            pool.wait_ge(const_step, 2)
            pool.affine_select(out=ident[:, :], in_=ident[:, :], compare_op=ALU.not_equal, fill=1.0,
                               base=0, pattern=[[-1, P]], channel_multiplier=1)
            pool.affine_select(out=earlier[:, :], in_=earlier[:, :], compare_op=ALU.is_ge, fill=0.0,
                               base=-1, pattern=[[1, P]], channel_multiplier=-1).then_inc(const_ready, 1)

            def rstd_of(n):
                lo, hi = NM * NORMS[n], NM * NORMS[n + 1]
                pool.wait_ge(mv1_ready, hi)
                pool.tensor_scalar(var1[:, lo:hi], mv1[:, lo:hi, 1], EPS, None, ALU.add).then_inc(rstd1_step, 1)
                pool.wait_ge(rstd1_step, n + 1)
                pool.tensor_tensor(rstd1[:, lo:hi], var1[:, lo:hi], minus_half[:, lo:hi], ALU.pow)\
                    .then_inc(rstd1_ready, 1)

            rstd_of(0)
            pool.memset(loss_w[:, :], -LR / (CT * D))
            pool.memset(ones[:, :], 1.0)
            pool.memset(before_all[:, 0], 0.0)
            pool.memset(nowhere[:, :, :], NOWHERE)
            pool.memset(rows[:, :, :, :, P:ROW], 0.0).then_inc(const_ready, 1)
            steps = [2]

            def stepped(ins):
                steps[0] += 1
                ins.then_inc(const_step, 1)
                pool.wait_ge(const_step, steps[0])

            stepped(pool.memset(same_or_earlier_row[:, :], 1.0))
            stepped(pool.memset(earlier_row[:, :], 0.0))
            stepped(pool.memset(same_or_earlier_row[CHUNK:P, 0:CHUNK], 0.0))
            stepped(pool.memset(earlier_row[0:CHUNK, CHUNK:P], 1.0))
            stepped(pool.iota(ints[:, 0:NM * TOP * E], pattern=[[0, NM * TOP], [1, E]], base=0, channel_multiplier=0))
            stepped(pool.tensor_copy(expert_id[:, :, :].rearrange("p a e -> p (a e)"), ints[:, 0:NM * TOP * E]))
            stepped(pool.iota(ints[:, 0:NM * E], pattern=[[0, NM], [CAP, E]], base=0, channel_multiplier=0))
            stepped(pool.tensor_copy(expert_base[:, :, :].rearrange("p m e -> p (m e)"), ints[:, 0:NM * E]))
            for h in range(2):
                stepped(pool.iota(ints[h * CHUNK:(h + 1) * CHUNK, :],
                                  pattern=[[TOP * CHUNK, NC], [TOP * 2 * S, NM], [1, TOP]],
                                  base=TOP * h * S, channel_multiplier=TOP))
            pool.tensor_copy(dest_id[:, :, :, :].rearrange("p c m k -> p (c m k)"), ints[:, :])\
                .then_inc(const_ready, 1)
            rstd_of(1)
            rstd_of(2)

            def spread(c, tiles):
                if c == 0:
                    pool.wait_ge(slots_blank, 16)
                pool.wait_ge(rows_ready, 2 * c + 2)
                pool.wait_ge(meta_ready, 2 * c + 2)
                pool.wait_ge(slot_ready, c + 1)
                for m in tiles:
                    for k in range(TOP):
                        n = m * TOP + k
                        pool.indirect_dma_start(
                            slots, bass.IndirectOffsetOnAxis(ap=slot_i[:, c, n:n + 1], axis=0),
                            rows[:, c % NR, m, k, :], None, bounds_check=E * CAP - 1, oob_is_err=False)\
                            .then_inc(rows_sent[c % NR], 16)

            def rstd2_of(c):
                pool.wait_ge(mv2_ready, 2 * c + 2)
                pool.tensor_scalar(var2[:, :], mv2[:, :, 1], EPS, None, ALU.add).then_inc(rstd2_step, 1)
                pool.wait_ge(rstd2_step, c + 1)
                if c > 0:
                    pool.wait_ge(z_ready, 2 * c)
                pool.tensor_tensor(rstd2[:, :], var2[:, :], minus_half[:, 0:NM], ALU.pow).then_inc(rstd2_ready, 1)
                if c < NC - 1:
                    pool.wait_ge(rstd2_ready, c + 1)
                    pool.wait_ge(minus_mean2_ready, c + 1)
                    pool.tensor_tensor(shift2[:, :], minus_mean2[:, :], rstd2[:, :], ALU.mult)\
                        .then_inc(shift2_ready, 1)

            def split_bias():
                pool.wait_ge(w_route, 32)
                left = rb_sb[:, :]
                for i in range(SPLIT):
                    stepped(pool.tensor_copy(rb_high[:, i, :], left))
                    if i < SPLIT - 1:
                        stepped(pool.tensor_tensor(rb_left[:, i, :], left, rb_high[:, i, :], ALU.subtract))
                        left = rb_left[:, i, :]
                for i in range(SPLIT):
                    stepped(pool.tensor_tensor(rb_part[:, i, :], rb_high[:, i, :],
                                               ident[0:SPLIT, i:i + 1].to_broadcast([SPLIT, E]), ALU.mult))
                stepped(pool.tensor_tensor(rb_sum[:, :], rb_part[:, 0, :], rb_part[:, 1, :], ALU.add))
                pool.tensor_tensor(rb_split[:, :], rb_sum[:, :], rb_part[:, 2, :], ALU.add).then_inc(bias_ready, 1)

            rstd2_of(0)
            split_bias()
            rstd_of(3)
            rstd2_of(1)
            for c in range(2, NC):
                spread(c - 2, (0,))
                rstd2_of(c)
                spread(c - 2, (1,))
            spread(NC - 2, range(NM))
            spread(NC - 1, range(NM))

            pool.wait_ge(overflow_ready, 1)
            flag = pool.value_load(overflow[0:1, 0:1], min_val=0, max_val=1)
            with pool.If(flag > 0):
                for r in range(NR):
                    pool.wait_ge(rows_sent[r], 16 * NM * TOP * (NC // NR))
                for n in range(T * TOP // CAP + 1):
                    lo, hi = n * CAP, min((n + 1) * CAP, T * TOP)
                    k = (hi - lo) // P
                    pool.dma_start(chosen[lo:hi, :].rearrange("(p j) d -> p j d", j=k), blank[:, 0:k, 0:P])\
                        .then_inc(cleared, 16)
                pool.wait_ge(cleared, 16 * (T * TOP // CAP + 1))
                for r in range(NR):
                    pool.wait_ge(rows_stored[r], 16 * (NC // NR))
                pool.wait_ge(late_slots, 1)
                with pool.Fori(0, NC) as c:
                    pool.dma_start(again_rows[:, :, :, :].rearrange("p m k r -> p (m k r)"),
                                   rows_kept[bass.ds(c, 1)].rearrange("o p n -> (o p) n")).then_inc(again_loaded, 16)
                    pool.tensor_copy(again_i[:, :], slot_il[:, bass.ds(c, 1)].rearrange("p o n -> p (o n)"))\
                        .then_inc(again_copied, 1)
                    pool.wait_ge(again_loaded, 16 * c + 16)
                    pool.wait_ge(again_copied, c + 1)
                    settle(pool, "pool")
                    for m in range(NM):
                        for k in range(TOP):
                            n = m * TOP + k
                            pool.indirect_dma_start(
                                slots, bass.IndirectOffsetOnAxis(ap=again_i[:, n:n + 1], axis=0),
                                again_rows[:, m, k, :], None, bounds_check=E * CAP - 1, oob_is_err=False)\
                                .then_inc(again_sent, 16)
                    pool.wait_ge(again_sent, 16 * NM * TOP * (c + 1))
                    settle(pool, "pool")
            pool.sem_inc(dispatched, 1)

            def send(e, q, pairs):
                for n, (lo, hi) in enumerate(DOWN):
                    pool.wait_ge(result_ready, 2 * e + n + 1)
                    settle(pool, "pool")
                    for j in range(lo, hi):
                        pool.indirect_dma_start(
                            chosen, bass.IndirectOffsetOnAxis(ap=dst[:, q, j:j + 1], axis=0),
                            result[:, q, j, :], None, bounds_check=T * TOP - 1, oob_is_err=False)\
                            .then_inc(result_sent[q], 16)

            by_expert(send)(pool, E)

        @block.scalar
        def _(act):
            act.preload_act_table(ACT.Silu)

            def turn_x(c):
                act.wait_ge(xT_in_psum, c + 1)
                act.copy(xnT_high[:, c, :], xT_ps(c)).then_inc(xT_high, 1)

            def norm_x(c):
                act.wait_ge(shift1_ready, c - BY_ACT + 1)
                for m in range(NM):
                    t = NM * c + m
                    act.activation(xn_all[:, c, m, :], x_all[:, c, m, :], ACT.Identity,
                                   scale=rstd1[:, t:t + 1], bias=shift1[:, t:t + 1]).then_inc(xn_rest, 1)

            def gate_up(c):
                act.wait_ge(s_ready, c + 1)
                for n in range(NF // 2):
                    act.wait_ge(g_ready, NF // 2 * c + n + 1)
                    act.activation(gated[:, 2 * n:2 * n + 2, :], gu[:, 0, 2 * n:2 * n + 2, :], ACT.Silu,
                                   scale=s_cur[:, c % 2:c % 2 + 1]).then_inc(gated_ready, 1)

            def normalise(c):
                if c >= NR:
                    act.wait_ge(rows_sent[c % NR], 16 * NM * TOP * (c // NR))
                    act.wait_ge(rows_stored[c % NR], 16 * (c // NR))
                act.wait_ge(shift2_ready, c + 1)
                act.wait_ge(rstd2_ready, c + 1)
                for m in range(NM):
                    act.activation(rows[:, c % NR, m, 0, 0:P], x1_all[:, c, m, :], ACT.Identity,
                                   scale=rstd2[:, m:m + 1], bias=shift2[:, m:m + 1]).then_inc(z_ready, 1)

            def address(c):
                if c == 0:
                    act.wait_ge(const_ready, 3)
                if c < NC - 1:
                    act.wait_ge(z_ready, 2 * c + 2)
                else:
                    act.wait_ge(z_last, NM)
                act.copy(rows[:, c % NR, :, 1, 0:P], rows[:, c % NR, :, 0, 0:P]).then_inc(rows_ready, 1)
                act.copy(rows[:, c % NR, :, :, DEST], dest_id[:, c]).then_inc(rows_ready, 1)

            def turn_z(c):
                act.wait_ge(zT_in_psum, c + 1)
                act.copy(zT[:, :], zT_ps).then_inc(zT_ready, 1)

            def weigh(c):
                act.wait_ge(gap_ready, c + 1)
                act.activation(half_tanh[:, :], gap[:, :], ACT.Tanh, scale=0.5).then_inc(tanh_ready, 1)
                act.wait_ge(tanh_ready, c + 1)
                for k, sign in enumerate((0.5, -0.5)):
                    act.activation(rows[:, c % NR, :, k, GATE], half_tanh[:, :], ACT.Copy, scale=sign, bias=0.5)\
                        .then_inc(meta_ready, 1)

            def square(c):
                act.wait_ge(diff_ready, c + 1)
                act.activation(junk[:, :, :], diff[:, :, :], ACT.Square, accum_out=sq_sum[:, :]).then_inc(sq_ready, 1)

            def chunk(c):
                gate_up(c)
                if c == 0:
                    turn_x(1)
                    square(c)
                    turn_x(2)
                    return
                if c + 2 < NC:
                    turn_x(c + 2)
                if c >= 2:
                    weigh(c - 2)
                normalise(c - 1)
                address(c - 1)
                if BY_ACT <= c + 3 < NC:
                    norm_x(c + 3)
                turn_z(c - 1)
                if c < NC - 1:
                    square(c)

            act.wait_ge(xT_in_psum, 1)
            act.copy(xnT_first[:, :], xT_ps(0)).then_inc(xT_first, 1)
            act.wait_ge(w_up, 32)
            for a, w in enumerate((w0_sb, w2_sb)):
                act.copy(w_high[:, a, :], w[:, :]).then_inc(w_high_ready, 1)
            for c in range(NC):
                chunk(c)
            weigh(NC - 2)
            turn_z(NC - 1)
            address(NC - 1)
            weigh(NC - 1)
            act.preload_act_table(ACT.Gelu)
            act.wait_ge(b1_in_psum, 1)
            act.copy(b1T[:, :], b1T_ps).then_inc(b1_ready, 1)
            act.wait_ge(b1_ready, 1)

            def experts(e, q, pairs):
                for n, (lo, hi) in enumerate(HALVES):
                    for f in range(NEF):
                        act.wait_ge(hid_in_psum, 4 * e + 2 * n + f + 1)
                        settle(act, "act")
                        act.activation(hidden[:, f, lo:hi], hid_ps[:, 2 * n + f, 0:hi - lo], ACT.Gelu,
                                       bias=b1T[:, bass.ds(NEF * e + f, 1)]).then_inc(hid_ready, 1)

            by_expert(experts)(act, E)

        @block.vector
        def _(dve):
            dve.memset(warm[:, :], 0.0).then_inc(warm_ready, 1)
            dve.memset(s_cur[:, 0:1], 1.0).then_inc(s_ready, 1)
            dve.memset(s_sq[:, 0:1], 1.0).then_inc(s_sq_ready, 1)

            def norm1(n):
                lo, hi = NM * NORMS[n], NM * NORMS[n + 1]
                for t in range(lo, hi):
                    dve.bn_stats(stats1[:, t, :], x_all[:, t // NM, t % NM, :]).then_inc(ln1_step, 1)
                for t in range(lo, hi):
                    dve.wait_ge(ln1_step, t + 1)
                    dve.bn_aggr(mv1[:, t, :], stats1[:, t, :]).then_inc(mv1_ready, 1)

            def norm_x(c):
                for t in range(NM * c, NM * c + NM):
                    dve.tensor_scalar(xn_all[:, c, t % NM, :], x_all[:, c, t % NM, :], mv1[:, t, 0:1],
                                      rstd1[:, t:t + 1], ALU.subtract, ALU.mult).then_inc(xn_first, 1)

            def shift_x(lo, hi):
                part = slice(NM * lo, NM * hi)
                dve.scalar_tensor_tensor(out=shift1[:, part], in0=mv1[:, part, 0], scalar=-1.0,
                                         in1=rstd1[:, part], op0=ALU.mult, op1=ALU.mult).then_inc(shift1_ready, hi - lo)

            dve.wait_ge(x_first, 32)
            norm1(0)
            dve.wait_ge(rstd1_ready, 1)
            dve.wait_ge(mv1_ready, NM)
            norm_x(0)
            dve.wait_ge(x_soon, 16 * B)
            norm1(1)
            for a, w in enumerate((w0_sb, w2_sb)):
                dve.wait_ge(w_high_ready, a + 1)
                dve.tensor_tensor(w_rest[:, a, :], w[:, :], w_high[:, a, :].bitcast(F32), ALU.subtract)\
                    .then_inc(w_ready, 1)

            def rest_of(c):
                dve.wait_ge(xT_high, c)
                dve.tensor_tensor(xnT_rest[:, c, :], xT_ps(c), xnT_high[:, c, :].bitcast(F32), ALU.subtract)\
                    .then_inc(xT_ready, 1)

            def choose(c):
                dve.wait_ge(logits_in_psum, c + 1)
                for m in range(NM):
                    dve.max(best[:, m, :], logits_ps[:, m, :]).then_inc(best_ready, 1)

            def gap_of(c):
                dve.wait_ge(best_ready, 2 * c + 2)
                if c > 0:
                    dve.wait_ge(tanh_ready, c)
                dve.tensor_tensor(gap[:, :], best[:, :, 0], best[:, :, 1], ALU.subtract).then_inc(gap_ready, 1)

            def index_of(c):
                dve.wait_ge(best_ready, 2 * c + 2)
                for m in range(NM):
                    dve.max_index(best_id[:, m, :], best[:, m, :], logits_ps[:, m, :]).then_inc(best_id_ready, 1)

            def pick_of(c):
                dve.wait_ge(best_id_ready, 2 * c + 2)
                if c == 0:
                    dve.wait_ge(const_ready, 3)
                dve.tensor_tensor(pick_all[:, c], expert_id[:, :, :].rearrange("p (m k) e -> p m k e", k=TOP),
                                  best_id[:, :, 0:TOP].rearrange("p m (k o) -> p m k o", o=1)
                                  .to_broadcast([P, NM, TOP, E]), ALU.is_equal).then_inc(pick_ready, 1)
                dve.wait_ge(pick_ready, c + 1)
                dve.tensor_tensor(mask_all[:, c], pick_all[:, c, :, 0, :], pick_all[:, c, :, 1, :], ALU.add)\
                    .then_inc(mask_ready, 1)

            def count_picks(c):
                dve.wait_ge(mask_ready, c + 1)
                if c > 0:
                    dve.wait_ge(before_ready, c)
                dve.tensor_tensor(before_all[:, c + 1], before_all[:, c], mask_all[:, c], ALU.add)\
                    .then_inc(before_ready, 1)

            def place(c):
                s = 4 * c
                dve.wait_ge(pos_ready, c + 1)
                dve.scalar_tensor_tensor(out=over[:, :, :], in0=pos_ps, scalar=CAP - 0.5, in1=nowhere[:, 0:NM, :],
                                         op0=ALU.is_gt, op1=ALU.mult).then_inc(slot_step, 1)
                dve.tensor_tensor(based[:, :, :], pos_ps, expert_base[:, :, :], ALU.add).then_inc(slot_step, 1)
                dve.wait_ge(slot_step, s + 2)
                dve.tensor_tensor(slot_of[:, :, :], over[:, :, :], based[:, :, :], ALU.add).then_inc(slot_step, 1)
                dve.wait_ge(slot_step, s + 3)
                for k in range(TOP):
                    dve.tensor_tensor(slot_pick[:, :, k, :], pick_all[:, c, :, k, :], slot_of[:, :, :], ALU.mult)\
                        .then_inc(slot_picked, 1)
                dve.wait_ge(slot_picked, 2 * c + 2)
                dve.tensor_reduce(slot_f[:, :], slot_pick[:, :, :, :].rearrange("p m k e -> p (m k) e"), AX.X, ALU.add)\
                    .then_inc(slot_step, 1)
                dve.wait_ge(slot_step, s + 4)
                dve.tensor_copy(slot_i[:, c, :], slot_f[:, :]).then_inc(slot_ready, 1)

            def chunk(c):
                q, last = c % 2, c == NC - 1
                for n in range(NF // 2):
                    dve.wait_ge(u_ready, NF // 2 * c + n + 1)
                    dve.wait_ge(gated_ready, NF // 2 * c + n + 1)
                    dve.tensor_tensor(prod[:, 2 * n:2 * n + 2, :], gated[:, 2 * n:2 * n + 2, :],
                                      gu[:, 1, 2 * n:2 * n + 2, :], ALU.mult).then_inc(prod_ready, 1)
                    if c == 0:
                        if n == 0:
                            dve.wait_ge(rstd1_ready, 2)
                            dve.wait_ge(mv1_ready, NM * NORMS[2])
                        norm_x(n + 1)
                    if n == 0 and c >= 2:
                        pick_of(c - 2)
                if c >= 2:
                    count_picks(c - 2)
                if c + 2 < NC:
                    rest_of(c + 2 if c else 1)
                if c == 0:
                    dve.wait_ge(x_rest, 16 * B)
                    norm1(2)
                if c == 1:
                    norm1(3)
                if c >= 2:
                    place(c - 2)
                dve.wait_ge(out_ready, c + 1)
                dve.wait_ge(s_sq_ready, c + 1)
                dve.wait_ge(xn_first, NM * min(c + 1, BY_ACT))
                if c >= BY_ACT:
                    dve.wait_ge(xn_rest, NM * (c + 1 - BY_ACT))
                if not last:
                    dve.scalar_tensor_tensor(out=diff[:, :, :], in0=out_ps, scalar=s_sq[:, q:q + 1], in1=xn_all[:, c],
                                             op0=ALU.mult, op1=ALU.subtract).then_inc(diff_ready, 1)
                dve.scalar_tensor_tensor(out=x1_all[:, c], in0=out_ps, scalar=s_sq[:, q:q + 1], in1=x_all[:, c],
                                         op0=ALU.mult, op1=ALU.add).then_inc(x1_ready, 1)
                dve.wait_ge(x1_ready, c + 1)
                for m in range(NM):
                    dve.bn_stats(stats2[:, m, :], x1_all[:, c, m, :]).then_inc(stats2_done, 1)
                if not last:
                    dve.wait_ge(loss_ready, c + 1)
                    dve.scalar_tensor_tensor(out=s_cur[:, 1 - q:2 - q], in0=loss_ps, scalar=1.0,
                                             in1=s_cur[:, q:q + 1], op0=ALU.add, op1=ALU.mult).then_inc(s_ready, 1)
                if c > 0:
                    dve.wait_ge(shift2_ready, c)
                dve.wait_ge(stats2_done, 2 * c + 2)
                for m in range(NM):
                    dve.bn_aggr(mv2[:, m, :], stats2[:, m, :]).then_inc(mv2_ready, 1)
                if not last:
                    dve.wait_ge(s_ready, c + 2)
                    dve.tensor_tensor(s_sq[:, 1 - q:2 - q], s_cur[:, 1 - q:2 - q], s_cur[:, 1 - q:2 - q], ALU.mult)\
                        .then_inc(s_sq_ready, 1)
                if not last:
                    dve.wait_ge(mv2_ready, 2 * c + 2)
                    dve.tensor_scalar(minus_mean2[:, :], mv2[:, :, 0], -1.0, None, ALU.mult)\
                        .then_inc(minus_mean2_ready, 1)
                if c > 0:
                    choose(c - 1)
                    gap_of(c - 1)
                    index_of(c - 1)
                if c == 1:
                    dve.wait_ge(rstd1_ready, 4)
                    dve.wait_ge(mv1_ready, NM * NORMS[4])
                    shift_x(NORMS[3], NORMS[4])
                if c == 0:
                    dve.wait_ge(rstd1_ready, 3)
                    dve.wait_ge(mv1_ready, NM * NORMS[3])
                    norm_x(3)
                    shift_x(BY_ACT, NORMS[3])
                    rest_of(2)

            for c in range(NC):
                chunk(c)
            pick_of(NC - 2)
            count_picks(NC - 2)
            last_rows = (NC - 1) % NR
            dve.wait_ge(rows_sent[last_rows], 16 * NM * TOP * ((NC - 1) // NR))
            dve.wait_ge(rows_stored[last_rows], 16 * ((NC - 1) // NR))
            dve.wait_ge(rstd2_ready, NC)
            for m in range(NM):
                dve.tensor_scalar(rows[:, last_rows, m, 0, 0:P], x1_all[:, NC - 1, m, :], mv2[:, m, 0:1],
                                  rstd2[:, m:m + 1], ALU.subtract, ALU.mult).then_inc(z_last, 1)
            place(NC - 2)
            choose(NC - 1)
            gap_of(NC - 1)
            index_of(NC - 1)
            pick_of(NC - 1)
            count_picks(NC - 1)
            place(NC - 1)

            dve.wait_ge(count_ready, 1)
            dve.tensor_reduce(most[:, :], count_ps, AX.X, ALU.max).then_inc(most_ready, 1)
            dve.wait_ge(most_ready, 1)
            dve.tensor_scalar(overflow[:, :], most[:, :], CAP + 0.5, None, ALU.is_gt).then_inc(overflow_ready, 1)

            dve.wait_ge(before_ready, NC)
            total = before_all[:, NC:NC + 1].to_broadcast([P, NC, NM, E])
            dve.tensor_tensor(after_all[:, :, :, :], total, before_all[:, 0:NC], ALU.subtract).then_inc(after_step, 1)
            dve.wait_ge(after_step, 1)
            dve.tensor_tensor(after_all[:, :, :, :], after_all[:, :, :, :], mask_all[:, :, :, :], ALU.subtract)\
                .then_inc(after_ready, 1)
            dve.wait_ge(rank_ready, 1)
            ranks = rank_ps.rearrange("p c m e -> p (c m) e")
            dve.scalar_tensor_tensor(out=over_l[:, :, :], in0=ranks, scalar=CAP - 0.5, in1=nowhere[:, :, :],
                                     op0=ALU.is_gt, op1=ALU.mult).then_inc(late_step, 1)
            dve.tensor_tensor(based_l[:, :, :], ranks, expert_base[:, 0:1, :].to_broadcast([P, NC * NM, E]), ALU.add)\
                .then_inc(late_step, 1)
            dve.wait_ge(late_step, 2)
            dve.tensor_tensor(over_l[:, :, :], over_l[:, :, :], based_l[:, :, :], ALU.add).then_inc(late_step, 1)
            dve.wait_ge(late_step, 3)
            for k in range(TOP):
                dve.tensor_tensor(pick_l[:, :, k, :], pick_all[:, :, :, k, :].rearrange("p c m e -> p (c m) e"),
                                  over_l[:, :, :], ALU.mult).then_inc(late_step, 1)
            dve.wait_ge(late_step, 5)
            dve.tensor_reduce(slot_fl[:, :], pick_l[:, :, :, :].rearrange("p a k e -> p (a k) e"), AX.X, ALU.add)\
                .then_inc(late_step, 1)
            dve.wait_ge(late_step, 6)
            dve.tensor_copy(slot_il[:, :, :].rearrange("p c n -> p (c n)"), slot_fl[:, :]).then_inc(late_slots, 1)

            def take_slots(e):
                for n, (lo, hi) in enumerate(HALVES):
                    dve.wait_ge(xsT_in_psum, 2 * e + n + 1)
                    dve.tensor_copy(xsT[:, lo:hi], xsT_ps[:, n, 0:hi - lo]).then_inc(xsT_ready, 1)

            def expert(e, q, pairs):
                if not (first(e) or last_expert(e)):
                    take_slots(e + 1)
                dve.wait_ge(xs_loaded[q], 16 * pairs + 16)
                if pairs_before(e):
                    dve.wait_ge(result_sent[q], 16 * NJ * pairs)
                dve.tensor_copy(dst[:, q, :], xs[:, q, :, DEST]).then_inc(xs_read, 1)
                dve.tensor_copy(wgt[:, q, :], xs[:, q, :, GATE]).then_inc(xs_read, 1)
                dve.wait_ge(xs_read, 2 * e + 2)
                for n, (lo, hi) in enumerate(DOWN):
                    dve.wait_ge(eo_in_psum, 2 * e + n + 1)
                    dve.tensor_tensor(biased[:, lo:hi, :], eo_ps[:, n, 0:hi - lo, :],
                                      b2_sb[:, bass.ds(e, 1)].to_broadcast([P, hi - lo, P]), ALU.add)\
                        .then_inc(biased_ready, 1)
                    dve.wait_ge(biased_ready, 2 * e + n + 1)
                    dve.tensor_tensor(result[:, q, lo:hi, :], biased[:, lo:hi, :],
                                      wgt[:, q, lo:hi].rearrange("p (j o) -> p j o", o=1).to_broadcast([P, hi - lo, P]),
                                      ALU.mult).then_inc(result_ready, 1)
                    if n == 0 and first(e):
                        take_slots(e + 1)

            dve.wait_ge(b_exp, 32)
            take_slots(0)
            by_expert_ahead(expert)(dve, E)

            for n, (m, lo, hi) in enumerate(PIECES):
                dve.wait_ge(picked_loaded[n], 32)
                dve.tensor_tensor(summed[:, m, lo:hi], picked[:, m, lo:hi, 0:P], picked[:, m, lo:hi, P:2 * P], ALU.add)\
                    .then_inc(summed_ready, 1)
                dve.wait_ge(summed_ready, n + 1)
                dve.tensor_tensor(final[:, m, lo:hi], summed[:, m, lo:hi], x1_all[:, lo:hi, m, :], ALU.add)\
                    .then_inc(final_ready, 1)

        @block.tensor
        def _(pe):
            def keep_warm(bank, count):
                for _ in range(count):
                    pe.matmul(bank, warm[:, 0:P], warm[:, :], start=True, stop=True)

            pe.wait_ge(warm_ready, 1)
            keep_warm(outp[:, 0, :], 12)
            pe.wait_ge(const_ready, 1)

            def turn_x(c):
                if c < BY_ACT:
                    pe.wait_ge(xn_first, NM * (c + 1))
                else:
                    pe.wait_ge(xn_rest, NM * (c + 1 - BY_ACT))
                if c == 2:
                    pe.wait_ge(xT_first, 1)
                if c > 2:
                    pe.wait_ge(xT_ready, c - 1)
                if c >= 4:
                    pe.wait_ge(zT_ready, c - 3)
                for m in range(NM):
                    t = pe.transpose(xT_ps(c)[:, m * P:(m + 1) * P], xn_all[:, c, m, :], ident[:, :])
                t.then_inc(xT_in_psum, 1)

            def up(c, a, n):
                for f in (2 * n, 2 * n + 1):
                    part = slice(f * P, (f + 1) * P)
                    if c == 0:
                        mm = pe.matmul(gu[:, a, f, :], (w0_sb, w2_sb)[a][:, part], xnT_first[:, :],
                                       start=True, stop=True)
                    else:
                        pe.matmul(gu[:, a, f, :], w_high[:, a, part], xnT_high[:, c, :], start=True, stop=False)
                        pe.matmul(gu[:, a, f, :], w_high[:, a, part], xnT_rest[:, c, :], start=False, stop=False)
                        mm = pe.matmul(gu[:, a, f, :], w_rest[:, a, part], xnT_high[:, c, :], start=False, stop=True)
                mm.then_inc((g_ready, u_ready)[a], 1)

            def down(c):
                for m in range(NM):
                    for f in range(NF):
                        if m == 0 and f % 2 == 0:
                            pe.wait_ge(prod_ready, NF // 2 * c + f // 2 + 1)
                        mm = pe.matmul(out_ps[:, m, :], prod[:, f, m * P:(m + 1) * P], w1_sb[:, f, :],
                                       start=(f == 0), stop=(f == NF - 1))
                mm.then_inc(out_ready, 1)

            def loss(c):
                pe.wait_ge(sq_ready, c + 1)
                pe.matmul(loss_ps, loss_w[:, :], sq_sum[:, :], start=True, stop=True).then_inc(loss_ready, 1)

            def turn_z(c):
                if c < NC - 1:
                    pe.wait_ge(z_ready, 2 * c + 2)
                else:
                    pe.wait_ge(z_last, NM)
                pe.wait_ge(xT_ready, min(c + 3, NC - 1))
                for m in range(NM):
                    t = pe.transpose(zT_ps[:, m * P:(m + 1) * P], rows[:, c % NR, m, 0, 0:P], ident[:, :])
                t.then_inc(zT_in_psum, 1)

            def route(c):
                if c == 0:
                    pe.wait_ge(w_route, 32)
                    pe.wait_ge(bias_ready, 1)
                if c > 0:
                    pe.wait_ge(slot_step, 4 * c)
                pe.matmul(logits_ps, ones[0:SPLIT, :], rb_split[:, :].rearrange("p (o e) -> p o e", o=1)
                          .to_broadcast([SPLIT, NM, E]), start=True, stop=False)
                pe.wait_ge(zT_ready, c + 1)
                for m in range(NM):
                    mm = pe.matmul(logits_ps[:, m, :], zT[:, m * P:(m + 1) * P], rw_sb[:, :],
                                   start=False, stop=(m == NM - 1))
                mm.then_inc(logits_in_psum, 1)

            def position(c):
                pe.wait_ge(mask_ready, c + 1)
                if c > 0:
                    pe.wait_ge(before_ready, c)
                mask, before = mask_all[:, c], before_all[:, c]
                pe.matmul(pos_ps, earlier[:, :], mask, start=True, stop=False)
                for m in range(NM):
                    pe.matmul(pos_ps, ones[:, :], before[:, m:m + 1, :].to_broadcast([P, NM, E]),
                              start=False, stop=False)
                pe.matmul(pos_ps[:, 1, :], ones[:, :], mask[:, 0, :], start=False, stop=True)\
                    .then_inc(pos_ready, 1)

            def chunk(c):
                up(c, 1, 0)
                up(c, 0, 1)
                if c >= 2:
                    loss(c - 1)
                    route(c - 2)
                up(c, 1, 1)
                if c == 0:
                    turn_x(1)
                    pe.wait_ge(w_down, 16)
                    down(0)
                    pe.wait_ge(xT_ready, 1)
                    pe.wait_ge(w_ready, 2)
                    up(1, 0, 0)
                    loss(0)
                    turn_x(2)
                    return
                if c + 2 < NC:
                    turn_x(c + 2)
                if c + 1 < NC:
                    pe.wait_ge(xT_ready, c + 1)
                    pe.wait_ge(gated_ready, NF // 2 * c + 1)
                    up(c + 1, 0, 0)
                if c >= 2:
                    position(c - 2)
                pe.wait_ge(x1_ready, c)
                down(c)
                turn_z(c - 1)

            turn_x(0)
            pe.wait_ge(xT_first, 1)
            pe.wait_ge(w_up, 32)
            up(0, 0, 0)
            for c in range(NC):
                chunk(c)
            route(NC - 2)
            position(NC - 2)
            turn_z(NC - 1)
            route(NC - 1)
            pe.wait_ge(b_exp, 32)
            pe.transpose(b1T_ps, b1_rows[:, :], ident[0:E * NEF, 0:E * NEF]).then_inc(b1_in_psum, 1)
            position(NC - 1)

            pe.wait_ge(before_ready, NC)
            for m in range(NM):
                mm = pe.matmul(count_ps, ones[:, :], before_all[:, NC, m, :], start=(m == 0), stop=(m == NM - 1))
            mm.then_inc(count_ready, 1)
            pe.matmul(rank_ps, earlier[:, :], mask_all[:, :, :, :], start=True, stop=False)
            pe.matmul(rank_ps, same_or_earlier_row[:, :], before_all[:, 0:NC], start=False, stop=False)
            pe.wait_ge(after_ready, 1)
            pe.matmul(rank_ps, earlier_row[:, :], after_all[:, :, :, :], start=False, stop=False)
            pe.matmul(rank_ps[:, :, 1, :], ones[:, :], before_all[:, NC, 0:1, :].to_broadcast([P, NC, E]),
                      start=False, stop=True).then_inc(rank_ready, 1)

            def turn_slots(e, q, pairs):
                if first(e):
                    pe.wait_ge(xs_begun, 16)
                    pe.wait_ge(late_slots, 1)
                    pe.wait_ge(overflow_ready, 1)
                    pe.wait_ge(b1_ready, 1)
                for n, (lo, hi) in enumerate(DOWN):
                    if not (first(e) and n == 0):
                        pe.wait_ge(xs_loaded[q], 16 * pairs + 16)
                    for j in range(lo, hi):
                        t = pe.transpose(xsT_ps[:, n, (j - lo) * P:(j - lo + 1) * P], xs[:, q, j, 0:P], ident[:, :])
                    t.then_inc(xsT_in_psum, 1)

            def expert(e, q, pairs):
                pe.wait_ge(we_loaded[q], 32 * pairs + 32)
                for n, (lo, hi) in enumerate(HALVES):
                    pe.wait_ge(xsT_ready, 2 * e + n + 1)
                    for f in range(NEF):
                        pe.matmul(hid_ps[:, 2 * n + f, 0:hi - lo], we1_sb[:, q, f * P:(f + 1) * P], xsT[:, lo:hi],
                                  start=True, stop=True).then_inc(hid_in_psum, 1)
                nxt = (e + 1, 1 - q, pairs + q)
                if not (first(e) or last_expert(e)):
                    turn_slots(*nxt)
                for n, (lo, hi) in enumerate(DOWN):
                    pe.wait_ge(hid_ready, 4 * e + 2 * n + 2)
                    if n == 0 and not first(e):
                        pe.wait_ge(biased_ready, 2 * e)
                    for j in range(lo, hi):
                        for f in range(NEF):
                            mm = pe.matmul(eo_ps[:, n, j - lo, :], hidden[:, f, j * P:(j + 1) * P], we2_sb[:, q, f, :],
                                           start=(f == 0), stop=(f == NEF - 1))
                    mm.then_inc(eo_in_psum, 1)
                    if n == 0 and first(e):
                        turn_slots(*nxt)

            keep_warm(hid_ps[:, 0, :], 30)
            turn_slots(0, 0, 0)
            by_expert_ahead(expert)(pe, E)


_INS = ['L0_attn_x', 'L0_attn_w0', 'L0_attn_w1', 'L0_attn_w2', 'L0_ffn_router_w', 'L0_ffn_router_b',
        'L0_ffn_w1', 'L0_ffn_b1', 'L0_ffn_w2', 'L0_ffn_b2']
_OUTS = [((4, 512, 128), 'float32')]


def kernel(**inputs):
    import numpy as _np
    import concourse.bacc as _bacc
    from concourse import mybir as _mybir
    from concourse.bass_utils import run_bass_kernel_spmd as _run

    nc = _bacc.Bacc("TRN2", target_bir_lowering=False, num_devices=1)
    arrays, args = {}, []
    for name in _INS:
        a = _np.ascontiguousarray(inputs[name])
        arrays[f"in_{name}_dram"] = a
        args.append(nc.dram_tensor(f"in_{name}_dram", a.shape, _mybir.dt.from_np(a.dtype), kind="ExternalInput").ap())
    for i, (shape, dtype) in enumerate(_OUTS):
        dt = _mybir.dt.from_np(_np.dtype(dtype))
        args.append(nc.dram_tensor(f"out_{i}_dram", shape, dt, kind="ExternalOutput").ap())
    block_kernel(nc, *args)
    r = _run(nc, [arrays], core_ids=[0])
    got = tuple(r.results[0][f"out_{i}_dram"] for i in range(len(_OUTS)))
    return got[0]
```
